# Optimizing a Trainium2 kernel written in Bass

```python
import numpy as np
import jax
import jax.numpy as jnp

def _softmax(x, axis=-1):
    return jax.nn.softmax(x, axis=axis)

def _gelu(x):
    return jax.nn.gelu(x, approximate=True)

def _silu(x):
    return jax.nn.silu(x)

def _sigmoid(x):
    return jax.nn.sigmoid(x)

def _layernorm(x, axis=-1, eps=1e-05):
    m = jnp.mean(x, axis=axis, keepdims=True)
    v = jnp.var(x, axis=axis, keepdims=True)
    return (x - m) / jnp.sqrt(v + eps)

def _scatter_add(tgt, idx, src, axis=0):
    return tgt.at[idx].add(src)

def _segment_sum(src, seg, n):
    return jax.ops.segment_sum(src, seg, n)
kernel_name = 'mk_xattn_ffn_d2_seqx_r8_5a8808'

def setup_inputs(seed: int=0):
    np.random.seed(seed)
    _w = jnp.asarray

    def _rec_inputs():
        import jax
        import jax.numpy as jnp
        _rk = jax.random.key(seed)
        x = -0.0002928 + 1 * jax.random.normal(jax.random.fold_in(_rk, 1), (32, 128, 128), jnp.float32)
        _lenS = 128 - jax.random.randint(jax.random.fold_in(_rk, 7), (32,), 0, max(1, 128 // 4) + 1, jnp.int32)
        _lenS2 = 128 - jax.random.randint(jax.random.fold_in(_rk, 8), (32,), 0, max(1, 128 // 4) + 1, jnp.int32)
        _ctx_1024P = jax.random.normal(jax.random.fold_in(_rk, 11), (32, 16, 128), jnp.float32)
        _ctx_1024c = jax.random.dirichlet(jax.random.fold_in(_rk, 511), 0.3 * jnp.ones((16,), jnp.float32), (32, 128))
        _ctx_1024t = jnp.einsum('bsk,bkd->bsd', _ctx_1024c, _ctx_1024P)
        _ctx_1024t = _ctx_1024t * jax.lax.rsqrt(jnp.mean(jnp.square(_ctx_1024t)) + 1e-12) * 0.953939
        ctx_1024 = -1.39393e-06 + 0.999914 * (_ctx_1024t + 0.3 * jax.random.normal(jax.random.fold_in(_rk, 611), (32, 128, 128), jnp.float32))
        return (x, ctx_1024)
    x, ctx_1024 = _rec_inputs()

    def _L0_xattn_setup():
        import jax, jax.numpy as jnp
        import numpy as np
        D_MODEL = 128
        N_HEADS = 16
        D_K = D_MODEL // N_HEADS
        ROPE_BASE = 10000.0

        def rope_cos_sin(seq_len, d_k, base=ROPE_BASE, dtype=jnp.float32):
            inv_freq = 1.0 / base ** (jnp.arange(0, d_k, 2, dtype=dtype) / d_k)
            pos = jnp.arange(seq_len, dtype=dtype)
            freqs = jnp.outer(pos, inv_freq)
            return (jnp.cos(freqs), jnp.sin(freqs))

        def apply_rope(x, cos, sin):
            x1 = x[..., 0::2]
            x2 = x[..., 1::2]
            c = cos[None, None]
            s = sin[None, None]
            r1 = x1 * c - x2 * s
            r2 = x1 * s + x2 * c
            return jnp.stack([r1, r2], axis=-1).reshape(x.shape)
        key = jax.random.key(seed)
        ks = jax.random.split(key, 7)
        B, T = (2, 256)
        q = jax.random.normal(ks[0], (B, T, D_MODEL), dtype=jnp.float32)
        k = jax.random.normal(ks[1], (B, T, D_MODEL), dtype=jnp.float32)
        v = jax.random.normal(ks[2], (B, T, D_MODEL), dtype=jnp.float32)
        scale = 1.0 / np.sqrt(D_MODEL)
        W_q = jax.random.normal(ks[3], (D_MODEL, D_MODEL), dtype=jnp.float32) * scale
        W_k = jax.random.normal(ks[4], (D_MODEL, D_MODEL), dtype=jnp.float32) * scale
        W_v = jax.random.normal(ks[5], (D_MODEL, D_MODEL), dtype=jnp.float32) * scale
        W_o = jax.random.normal(ks[6], (D_MODEL, D_MODEL), dtype=jnp.float32) * scale
        return {'q': q, 'k': k, 'v': v, 'W_q': W_q, 'W_k': W_k, 'W_v': W_v, 'W_o': W_o}
    _L0_xattn_all = _L0_xattn_setup()
    _L0_xattn_in = {k: v for k, v in _L0_xattn_all.items() if k in ('W_q', 'W_k', 'W_v', 'W_o')}
    del _L0_xattn_all

    def _L0_ffn_setup():
        import jax, jax.numpy as jnp
        import numpy as np
        EPS = 1e-05
        HEADS = 8
        DIM_KEY = 128
        K = 16
        NUM_KEYS = 32
        key = jax.random.key(seed)
        ks = jax.random.split(key, 5)
        B, T, D = (1, 128, 128)
        x = jax.random.normal(ks[0], (B, T, D), dtype=jnp.float32)
        norm_w = jnp.ones((D,), dtype=jnp.float32)
        wq = jax.random.normal(ks[1], (D, DIM_KEY * HEADS * 2), dtype=jnp.float32) * 0.02
        keys = jax.random.normal(ks[2], (HEADS, NUM_KEYS, 2, DIM_KEY), dtype=jnp.float32) * 0.02
        expert_down = jax.random.normal(ks[3], (NUM_KEYS * NUM_KEYS, D), dtype=jnp.float32) * 0.02
        expert_up = jax.random.normal(ks[4], (NUM_KEYS * NUM_KEYS, D), dtype=jnp.float32) * 0.02
        return {'x': x, 'norm_w': norm_w, 'wq': wq, 'keys': keys, 'expert_down': expert_down, 'expert_up': expert_up}
    _L0_ffn_all = _L0_ffn_setup()
    _L0_ffn_in = {k: v for k, v in _L0_ffn_all.items() if k in ('norm_w', 'wq', 'keys', 'expert_down', 'expert_up')}
    del _L0_ffn_all

    def _L1_xattn_setup():
        import jax, jax.numpy as jnp
        import numpy as np
        D_MODEL = 128
        NUM_HEADS = 16
        STRIDE_LIST = [1, 2, 4, 8, 1, 2, 4, 8, 1, 2, 4, 8, 1, 2, 4, 8]
        HEAD_DIM = D_MODEL // NUM_HEADS
        key = jax.random.key(seed)
        ks = jax.random.split(key, 8)
        B, T, S = (4, 128, 512)
        w_scale = 0.02
        return {'decoder_input': jax.random.normal(ks[0], (B, T, D_MODEL), jnp.float32), 'encoder_output': jax.random.normal(ks[1], (B, S, D_MODEL), jnp.float32), 'Wq': jax.random.normal(ks[2], (D_MODEL, D_MODEL), jnp.float32) * w_scale, 'bq': jnp.zeros((D_MODEL,), jnp.float32), 'Wk': jax.random.normal(ks[3], (D_MODEL, D_MODEL), jnp.float32) * w_scale, 'bk': jnp.zeros((D_MODEL,), jnp.float32), 'Wv': jax.random.normal(ks[4], (D_MODEL, D_MODEL), jnp.float32) * w_scale, 'bv': jnp.zeros((D_MODEL,), jnp.float32), 'Wo': jax.random.normal(ks[5], (D_MODEL, D_MODEL), jnp.float32) * w_scale, 'bo': jnp.zeros((D_MODEL,), jnp.float32)}
    _L1_xattn_all = _L1_xattn_setup()
    _L1_xattn_in = {k: v for k, v in _L1_xattn_all.items() if k in ('Wq', 'bq', 'Wk', 'bk', 'Wv', 'bv', 'Wo', 'bo')}
    del _L1_xattn_all

    def _L1_ffn_setup():
        import jax, jax.numpy as jnp
        import numpy as np
        INT8_MAX = 127.0

        def _absmax_scale(x, axes):
            amax = jnp.max(jnp.abs(x), axis=axes, keepdims=True)
            return jnp.maximum(amax, 1e-12) / INT8_MAX
        key = jax.random.key(seed)
        k1, k2 = jax.random.split(key)
        lhs = jax.random.normal(k1, (4, 1024, 128), dtype=jnp.float32)
        rhs = jax.random.normal(k2, (128, 128), dtype=jnp.float32)
        return {'lhs': lhs, 'rhs': rhs}
    _L1_ffn_all = _L1_ffn_setup()
    _L1_ffn_in = {k: v for k, v in _L1_ffn_all.items() if k in ('rhs',)}
    del _L1_ffn_all
    return {'x': x, 'ctx_1024': ctx_1024, 'L0_xattn_W_q': _L0_xattn_in['W_q'], 'L0_xattn_W_k': _L0_xattn_in['W_k'], 'L0_xattn_W_v': _L0_xattn_in['W_v'], 'L0_xattn_W_o': _L0_xattn_in['W_o'], 'L0_ffn_norm_w': _L0_ffn_in['norm_w'], 'L0_ffn_wq': _L0_ffn_in['wq'], 'L0_ffn_keys': _L0_ffn_in['keys'], 'L0_ffn_expert_down': _L0_ffn_in['expert_down'], 'L0_ffn_expert_up': _L0_ffn_in['expert_up'], 'L1_xattn_Wq': _L1_xattn_in['Wq'], 'L1_xattn_bq': _L1_xattn_in['bq'], 'L1_xattn_Wk': _L1_xattn_in['Wk'], 'L1_xattn_bk': _L1_xattn_in['bk'], 'L1_xattn_Wv': _L1_xattn_in['Wv'], 'L1_xattn_bv': _L1_xattn_in['bv'], 'L1_xattn_Wo': _L1_xattn_in['Wo'], 'L1_xattn_bo': _L1_xattn_in['bo'], 'L1_ffn_rhs': _L1_ffn_in['rhs']}

def reference(x, ctx_1024, L0_xattn_W_q, L0_xattn_W_k, L0_xattn_W_v, L0_xattn_W_o, L0_ffn_norm_w, L0_ffn_wq, L0_ffn_keys, L0_ffn_expert_down, L0_ffn_expert_up, L1_xattn_Wq, L1_xattn_bq, L1_xattn_Wk, L1_xattn_bk, L1_xattn_Wv, L1_xattn_bv, L1_xattn_Wo, L1_xattn_bo, L1_ffn_rhs):
    import jax
    import jax.numpy as jnp

    def _L0_xattn_ref(q, k, v, W_q, W_k, W_v, W_o):
        import jax, jax.numpy as jnp
        import numpy as np
        D_MODEL = 128
        N_HEADS = 16
        D_K = D_MODEL // N_HEADS
        ROPE_BASE = 10000.0

        def rope_cos_sin(seq_len, d_k, base=ROPE_BASE, dtype=jnp.float32):
            inv_freq = 1.0 / base ** (jnp.arange(0, d_k, 2, dtype=dtype) / d_k)
            pos = jnp.arange(seq_len, dtype=dtype)
            freqs = jnp.outer(pos, inv_freq)
            return (jnp.cos(freqs), jnp.sin(freqs))

        def apply_rope(x, cos, sin):
            x1 = x[..., 0::2]
            x2 = x[..., 1::2]
            c = cos[None, None]
            s = sin[None, None]
            r1 = x1 * c - x2 * s
            r2 = x1 * s + x2 * c
            return jnp.stack([r1, r2], axis=-1).reshape(x.shape)
        B, T_q, _ = q.shape
        T_k = k.shape[1]
        Q = (q @ W_q.T).reshape(B, T_q, N_HEADS, D_K).transpose(0, 2, 1, 3)
        K = (k @ W_k.T).reshape(B, T_k, N_HEADS, D_K).transpose(0, 2, 1, 3)
        V = (v @ W_v.T).reshape(B, T_k, N_HEADS, D_K).transpose(0, 2, 1, 3)
        cos_q, sin_q = rope_cos_sin(T_q, D_K)
        cos_k, sin_k = rope_cos_sin(T_k, D_K)
        Q = apply_rope(Q, cos_q, sin_q)
        K = apply_rope(K, cos_k, sin_k)
        scale = jnp.sqrt(jnp.asarray(D_K, dtype=Q.dtype))
        scores = jnp.einsum('bhqd,bhkd->bhqk', Q, K) / scale
        attn = jax.nn.softmax(scores, axis=-1)
        out = jnp.einsum('bhqk,bhkd->bhqd', attn, V)
        out = out.transpose(0, 2, 1, 3).reshape(B, T_q, D_MODEL)
        return out @ W_o.T

    def _L0_ffn_ref(x, norm_w, wq, keys, expert_down, expert_up):
        import jax, jax.numpy as jnp
        import numpy as np
        EPS = 1e-05
        HEADS = 8
        DIM_KEY = 128
        K = 16
        NUM_KEYS = 32
        B, T, D = x.shape
        inv = jax.lax.rsqrt(jnp.mean(x * x, axis=-1, keepdims=True) + EPS)
        x_norm = x * inv * norm_w
        q = (x_norm @ wq).reshape(B, T, HEADS, 2, DIM_KEY)
        sim = jnp.einsum('bthpd,hkpd->pbthk', q, keys)
        s1, i1 = jax.lax.top_k(sim[0], K)
        s2, i2 = jax.lax.top_k(sim[1], K)
        all_idx = (i1[..., :, None] * NUM_KEYS + i2[..., None, :]).reshape(B, T, HEADS, K * K)
        all_scores = (s1[..., :, None] + s2[..., None, :]).reshape(B, T, HEADS, K * K)
        final_scores, pk = jax.lax.top_k(all_scores, K)
        final_idx = jnp.take_along_axis(all_idx, pk, axis=-1)
        wd = expert_down[final_idx]
        wu = expert_up[final_idx]
        hidden = jnp.einsum('btd,bthkd->bthk', x_norm, wd)
        hidden = jax.nn.gelu(hidden, approximate=False)
        hidden = hidden * jax.nn.relu(final_scores)
        out = jnp.einsum('bthk,bthkd->btd', hidden, wu)
        return out

    def _L1_xattn_ref(decoder_input, encoder_output, Wq, bq, Wk, bk, Wv, bv, Wo, bo):
        import jax, jax.numpy as jnp
        import numpy as np
        D_MODEL = 128
        NUM_HEADS = 16
        STRIDE_LIST = [1, 2, 4, 8, 1, 2, 4, 8, 1, 2, 4, 8, 1, 2, 4, 8]
        HEAD_DIM = D_MODEL // NUM_HEADS
        B, T, _ = decoder_input.shape
        S = encoder_output.shape[1]
        Q = decoder_input @ Wq.T + bq
        K = encoder_output @ Wk.T + bk
        V = encoder_output @ Wv.T + bv
        Q = Q.reshape(B, T, NUM_HEADS, HEAD_DIM).transpose(0, 2, 1, 3)
        K = K.reshape(B, S, NUM_HEADS, HEAD_DIM).transpose(0, 2, 1, 3)
        V = V.reshape(B, S, NUM_HEADS, HEAD_DIM).transpose(0, 2, 1, 3)
        scale = 1.0 / HEAD_DIM ** 0.5
        head_outs = []
        for h in range(NUM_HEADS):
            s = STRIDE_LIST[h]
            K_h = K[:, h, ::s, :]
            V_h = V[:, h, ::s, :]
            scores = jnp.einsum('btd,bsd->bts', Q[:, h], K_h) * scale
            attn = jax.nn.softmax(scores, axis=-1)
            head_outs.append(jnp.einsum('bts,bsd->btd', attn, V_h))
        out = jnp.stack(head_outs, axis=2).reshape(B, T, D_MODEL)
        return out @ Wo.T + bo

    def _L1_ffn_ref(lhs, rhs):
        import jax, jax.numpy as jnp
        import numpy as np
        INT8_MAX = 127.0

        def _absmax_scale(x, axes):
            amax = jnp.max(jnp.abs(x), axis=axes, keepdims=True)
            return jnp.maximum(amax, 1e-12) / INT8_MAX
        lhs_scale = _absmax_scale(lhs, (2,))
        rhs_scale = _absmax_scale(rhs, (0,))
        q_lhs = jnp.clip(jnp.round(lhs / lhs_scale), -INT8_MAX, INT8_MAX).astype(jnp.int8)
        q_rhs = jnp.clip(jnp.round(rhs / rhs_scale), -INT8_MAX, INT8_MAX).astype(jnp.int8)
        acc = jax.lax.dot_general(q_lhs, q_rhs, (((2,), (0,)), ((), ())), preferred_element_type=jnp.int32)
        return acc.astype(jnp.float32) * lhs_scale * rhs_scale
    x = x + _L0_xattn_ref(_layernorm(x, axis=-1), ctx_1024, ctx_1024, L0_xattn_W_q, L0_xattn_W_k, L0_xattn_W_v, L0_xattn_W_o)
    x = x + _L0_ffn_ref(_layernorm(x, axis=-1), L0_ffn_norm_w, L0_ffn_wq, L0_ffn_keys, L0_ffn_expert_down, L0_ffn_expert_up)
    x = x + _L1_xattn_ref(_layernorm(x, axis=-1), ctx_1024, L1_xattn_Wq, L1_xattn_bq, L1_xattn_Wk, L1_xattn_bk, L1_xattn_Wv, L1_xattn_bv, L1_xattn_Wo, L1_xattn_bo)
    x = x + _L1_ffn_ref(_layernorm(x, axis=-1), L1_ffn_rhs)
    return x

_drawn_inputs = setup_inputs


def setup_inputs(seed=0):
    import zlib

    import numpy as np

    out = dict(_drawn_inputs(seed))
    spreads = {'L0_ffn_norm_w': (1.0, 0.6),
     'L1_xattn_bq': (0.0, 2.0),
     'L1_xattn_bk': (0.0, 2.0),
     'L1_xattn_bv': (0.0, 2.0),
     'L1_xattn_bo': (0.0, 2.0)}
    factors = {'L0_ffn_wq': 7.484,
     'L0_ffn_keys': 7.483,
     'L0_ffn_expert_down': 7.367,
     'L0_ffn_expert_up': 7.302,
     'L1_xattn_Wq': 64.0,
     'L1_xattn_Wk': 64.0,
     'L1_xattn_Wv': 8.0,
     'L1_xattn_Wo': 8.0}
    for name, (base, spread) in spreads.items():
        noise = np.random.default_rng([zlib.crc32(name.encode()), seed]).standard_normal(out[name].shape)
        drawn = base * np.exp(spread * noise) if base else spread * noise
        out[name] = jnp.asarray(drawn.astype(out[name].dtype))
    for name, factor in factors.items():
        out[name] = (out[name] * factor).astype(out[name].dtype)
    return out
```

```python
from contextlib import ExitStack

import concourse.bass as bass
from concourse import mybir

F32 = mybir.dt.float32
BF16 = mybir.dt.bfloat16
ALU = mybir.AluOpType
ACT = mybir.ActivationFunctionType
AX_X = mybir.AxisListType.X

P = 128
HEADS = 16
DK = P // HEADS
VW = DK + 1
GROUP = 4
GROUPS = HEADS // GROUP
STRIDES = (1, 2, 4, 8)
NK1 = [P // s for s in STRIDES]
OFF1 = [sum(NK1[:c]) for c in range(GROUP)]
W1 = sum(NK1)
EH = 8
NKEY = 32
TOP = 16
EXPERTS = NKEY * NKEY
EC = EXPERTS // P
PAIRS = [(0, 1, 16), (1, 1, 8), (2, 1, 5), (3, 1, 4), (4, 1, 3), (5, 3, 2), (8, 8, 1)]
NCAND = sum(a * b for _, a, b in PAIRS)
EPS = 1e-5
QMAX = 127.0
ROUND = 12582912.0
LOW = -3.0e38
SCALE = 1.0 / float(DK) ** 0.5

WQ0, WK0, WV0, WO0, WQ1, WK1, WV1, WO1 = range(8)
KEYS, SUBQ, DOWN, RHS = 8, 12, 28, 36
SLOTS = 37
C_ID, C_COS, C_SIN, C_MASK = 0, P, 3 * P, 5 * P
C_ALL = 5 * P + HEADS


def wait(eng, sem, value):
    if isinstance(value, int) and value <= 0:
        return
    eng.wait_ge(sem, value)


def hold(eng, sem, value, held):
    wait(eng, sem, value)
    eng.sem_inc(held, 1)


def build(nc, x, ctxt, wq0, wk0, wv0, wo0, norm_w, subq, keys, down, up,
          wq1, bq1, wk1, bk1, wv1, bv1, wo1, bo1, rhs, table, out):
    TILES = x.shape[0]

    with ExitStack() as stack:
        def sb(name, shape, dt=F32):
            return stack.enter_context(nc.sbuf_tensor(name, shape, dt))

        def bank(name, cols=512):
            return stack.enter_context(nc.psum_tensor(name, [P, cols], F32))

        def sem(name):
            return stack.enter_context(nc.semaphore(name))

        const = sb("const", [P, C_ALL])
        ident = const[:, C_ID:C_ID + P]
        cos_t = const[:, C_COS:C_COS + 2 * P]
        sin_t = const[:, C_SIN:C_SIN + 2 * P]
        hmask = const[:, C_MASK:C_MASK + HEADS]
        raw = sb("raw", [P, SLOTS, P])
        wt = sb("wt", [P, SLOTS, P])
        swapped = sb("swapped", [P, 2, P])
        w_sim = sb("w_sim", [P, 2 * EH * NKEY])
        down_t = sb("down_t", [P, EC, P])
        up_sb = sb("up_sb", [P, EC, P])
        cols = sb("cols", [P, 8])
        bv_rep = sb("bv_rep", [P, P])
        bo_rep = sb("bo_rep", [P, P])
        attn_bias = sb("attn_bias", [P, P])
        rhs_amax = sb("rhs_amax", [P, 4])
        rhs_r = sb("rhs_r", [P, P])
        rhs_srep = sb("rhs_srep", [P, P])
        rhs_q = sb("rhs_q", [P, P], BF16)
        rhs_row = sb("rhs_row", [P, P])
        neghalf = sb("neghalf", [P, 1])

        a_x = sb("a_x", [P, P])
        a_xres = sb("a_xres", [P, P])
        a_ctx = sb("a_ctx", [P, P])
        a_st = sb("a_st", [P, 6])
        a_mv = sb("a_mv", [P, 2])
        a_r = sb("a_r", [P, 2])
        a_xn = sb("a_xn", [P, P])
        a_xct = sb("a_xct", [P, 2 * P])
        a_v = sb("a_v", [P, HEADS, VW])
        a_ropec = sb("a_ropec", [P, 2 * P])
        a_ropes = sb("a_ropes", [P, 2 * P])
        a_qkt = sb("a_qkt", [P, 2 * P])
        a_kbd = sb("a_kbd", [P, HEADS, P])
        a_nmax = sb("a_nmax", [P, HEADS])
        a_p = sb("a_p", [P, 2, GROUP * P])
        a_pt = sb("a_pt", [P, 2, GROUP * P])
        a_rec = sb("a_rec", [P, HEADS])
        a_o = sb("a_o", [P, P])
        a_ot = sb("a_ot", [P, P])
        x1 = sb("x1", [P, P])
        b_x1 = sb("b_x1", [P, P])
        b_st = sb("b_st", [P, 6])
        b_mv = sb("b_mv", [P, 2])
        b_r = sb("b_r", [P, 8])
        b_xs = sb("b_xs", [P, P])
        b_xst = sb("b_xst", [P, P])
        b_g = sb("b_g", [P, EXPERTS])
        b_sim = sb("b_sim", [P, 2 * EH, NKEY])
        b_rest = sb("b_rest", [P, 2 * EH, NKEY])
        b_top = sb("b_top", [P, 2 * EH, TOP])
        b_cand = sb("b_cand", [P, EH, NCAND])
        b_crest = sb("b_crest", [P, EH, NCAND])
        b_ctop = sb("b_ctop", [P, EH, TOP])
        b_thr = sb("b_thr", [P, EH])
        NS = 3
        b_sum = sb("b_sum", [P, NS, EXPERTS])
        b_w = sb("b_w", [P, NS, EXPERTS])
        b_cg = sb("b_cg", [P, EXPERTS])
        x2 = sb("x2", [P, P])
        c_x2 = sb("c_x2", [P, P])
        c_ctx = sb("c_ctx", [P, P])
        c_st = sb("c_st", [P, 6])
        c_mv = sb("c_mv", [P, 2])
        c_r = sb("c_r", [P, 2])
        c_xn = sb("c_xn", [P, P])
        c_xct = sb("c_xct", [P, 2 * P])
        c_ctxc = sb("c_ctxc", [P, P])
        c_qt = sb("c_qt", [P, P])
        c_kt = sb("c_kt", [P, P])
        c_va = sb("c_va", [P, GROUPS, VW])
        c_vb = sb("c_vb", [P, GROUPS, 3, VW])
        c_kbd = sb("c_kbd", [P, GROUPS, W1])
        c_nmax = sb("c_nmax", [P, GROUP, GROUPS])
        c_p = sb("c_p", [P, GROUPS, 2 * P])
        c_pt = sb("c_pt", [P, 2, 4 * P])
        c_rec = sb("c_rec", [P, HEADS])
        c_o = sb("c_o", [P, P])
        c_ot = sb("c_ot", [P, P])
        c_x3 = sb("c_x3", [P, P])
        c_st3 = sb("c_st3", [P, 6])
        c_mv3 = sb("c_mv3", [P, 2])
        c_r3 = sb("c_r3", [P, 2])
        c_y = sb("c_y", [P, P])
        c_s = sb("c_s", [P, 3])
        c_yr = sb("c_yr", [P, P])
        c_yc = sb("c_yc", [P, P])
        c_yq = sb("c_yq", [P, P])
        c_yqt = sb("c_yqt", [P, P], BF16)
        c_d = sb("c_d", [P, P])
        c_out = sb("c_out", [P, P])

        M0 = bank("M0")
        M1 = bank("M1")
        SC = bank("SC", 1024)
        PT = bank("PT")
        H = bank("H", 1024)
        B0 = bank("B0")

        names = """w_loaded tr_done tr_copied w_ready sim_done bo_done rq_ready rq_done setup_pe setup_dve setup_pool
        a_xin a_xresin a_ctxin a_stat a_aggr a_eps a_rstd a_xn_ready a_tr a_xct_ready a_proj a_vproj a_vready a_rc a_rs
        a_qk_ready a_kbd_ready a_score a_max a_exp a_ptr a_ptcopy a_pv a_rec_ready a_o_ready a_otr a_ot_ready a_wo x1_ready
        b_kept b_stat b_aggr b_p1 b_p2 b_p3 b_p4 b_p5 b_p6 b_xs_ready b_tr b_xst_ready b_hid b_gelu b_simmm b_sim_ready
        b_t1 b_t2 b_t3 b_cand_ready b_c1 b_c2 b_c3 b_thr_ready b_sum_ready b_w_ready b_wtr b_cg_ready b_ffn x2_ready
        c_ctxin c_kept c_stat c_aggr c_eps c_rstd c_xn_ready c_tr c_xct_ready c_ctxc_ready c_qkproj c_vproj c_qt_ready
        c_v_ready c_kbd_ready c_score c_max c_exp c_ptr c_ptcopy c_pv c_rec_ready c_o_ready c_otr c_ot_ready c_wo
        c_x3_ready c_stat3 c_aggr3 c_eps3 c_rstd3 c_y_ready c_s1 c_s2 c_s3 c_yr_ready c_yc_ready c_yq_ready c_ytr
        c_yqt_ready c_int c_d_ready c_out_ready stored dve_held pool_held""".split()
        S = {n: sem(n) for n in names}

        block = stack.enter_context(nc.Block())

        def steps(eng, step):
            step(0, True, False, False)
            step(1, True, True, False)
            step(2, True, True, True)
            with eng.Fori(3, TILES) as s:
                step(s, True, True, True)
            step(TILES, False, True, True)
            step(TILES + 1, False, False, True)

        @block.sync
        def _(sp):
            weights = [(raw[:, WQ0 + i, :], w) for i, w in enumerate((wq0, wk0, wv0, wo0, wq1, wk1, wv1, wo1))]
            weights += [
                (const[:, :], table),
                (raw[:, KEYS:KEYS + 4, :], keys.rearrange("h k p d -> (h k p) d").rearrange("(c r) d -> r c d", r=P)),
                (raw[:, SUBQ:SUBQ + 16, :], subq.rearrange("i (c d) -> i c d", d=P)),
                (raw[:, DOWN:DOWN + EC, :], down.rearrange("(c r) d -> r c d", r=P)),
                (up_sb[:, :, :], up.rearrange("(c r) d -> r c d", r=P)),
                (raw[:, RHS, :], rhs),
                (cols[:, 0:1], norm_w.rearrange("(p a) -> p a", a=1)),
                (cols[:, 1:2], bq1.rearrange("(p a) -> p a", a=1)),
                (cols[:, 2:3], bk1.rearrange("(p a) -> p a", a=1)),
                (cols[:, 3:4], bv1.rearrange("(p a) -> p a", a=1)),
                (bo_rep[:, :], bo1.rearrange("(a n) -> a n", a=1).to_broadcast([P, P])),
            ]
            for to, of in weights:
                sp.dma_start(to, of).then_inc(S["w_loaded"], 16)
            assert len(weights) * 16 == LOADED

            def load_ctx(to, t, arrived):
                for at, first, stride in ((0, 0, 8), (16, 4, 8), (32, 2, 4), (64, 1, 2)):
                    n = P // stride
                    sp.dma_start(to[at:at + n, :],
                                 ctxt[t, :, :].rearrange("(n s) d -> s n d", s=stride)[first]).then_inc(arrived, 16)

            def step(s, A, B, C):
                if A:
                    t = s
                    wait(sp, S["a_xn_ready"], t)
                    sp.dma_start(a_x[:, :], x[t, :, :]).then_inc(S["a_xin"], 16)
                    wait(sp, S["a_tr"], t)
                    load_ctx(a_ctx, t, S["a_ctxin"])
                    wait(sp, S["x1_ready"], t)
                    sp.dma_start(a_xres[:, :], x[t, :, :]).then_inc(S["a_xresin"], 16)
                if C:
                    t = s - 2
                    wait(sp, S["c_tr"], t)
                    load_ctx(c_ctx, t, S["c_ctxin"])
                    sp.wait_ge(S["c_out_ready"], t + 1)
                    sp.dma_start(out[t, :, :], c_out[:, :]).then_inc(S["stored"], 16)
            steps(sp, step)
            sp.wait_ge(S["stored"], 16 * TILES)

        @block.tensor
        def _(pe):
            pe.wait_ge(S["w_loaded"], LOADED)
            banks = [M0[:, :], M1[:, :], PT[:, :], B0[:, :]]
            for r in range(ROUNDS):
                wait(pe, S["tr_copied"], r - 3)
                n = min(4, SLOTS - 4 * r)
                for j in range(n):
                    last = pe.transpose(banks[r % 4][:, j * P:(j + 1) * P], raw[:, 4 * r + j, :], ident)
                last.then_inc(S["tr_done"], 1)
            pe.wait_ge(S["tr_copied"], ROUNDS)
            for hp in range(2 * EH):
                h, half = hp // 2, hp % 2
                k0 = (h % 2) * 2 * NKEY + half
                last = pe.matmul(SC[:, hp * NKEY:(hp + 1) * NKEY], wt[:, SUBQ + hp, :],
                                 wt[:, KEYS + h // 2, k0:k0 + 2 * NKEY - 1:2], start=True, stop=True)
            last.then_inc(S["sim_done"], 1)
            pe.wait_ge(S["w_ready"], 1)
            pe.matmul(SC[:, 512:512 + P], bv_rep[:, :], wt[:, WO1, :], start=True, stop=True).then_inc(S["bo_done"], 1)
            pe.wait_ge(S["rq_ready"], 1)
            pe.transpose(H[:, 0:P], rhs_r[:, :], ident)
            pe.transpose(H[:, P:2 * P], rhs_srep[:, :], ident).then_inc(S["rq_done"], 1)
            pe.wait_ge(S["setup_dve"], 1)
            pe.wait_ge(S["setup_pool"], 4)

            def step(s, A, B, C):
                ta, tb, tc = s, s - 1, s - 2
                if A:
                    pe.wait_ge(S["a_xn_ready"], ta + 1)
                    pe.wait_ge(S["a_ctxin"], 64 * ta + 64)
                    wait(pe, S["c_yqt_ready"], tc)
                    pe.transpose(M0[:, 0:P], a_xn[:, :], ident)
                    pe.transpose(M0[:, P:2 * P], a_ctx[:, :], ident).then_inc(S["a_tr"], 1)
                if B:
                    pe.wait_ge(S["b_xs_ready"], tb + 1)
                    wait(pe, S["x2_ready"], tb)
                    pe.transpose(B0[:, 0:P], b_xs[:, :], ident).then_inc(S["b_tr"], 1)
                if A:
                    pe.wait_ge(S["a_xct_ready"], ta + 1)
                    wait(pe, S["c_d_ready"], tc)
                    for i, w in enumerate((wt[:, WQ0, :], wt[:, WK0, :], swapped[:, 0, :], swapped[:, 1, :])):
                        last = pe.matmul(M1[:, i * P:(i + 1) * P], w, a_xct[:, (i % 2) * P:(i % 2 + 1) * P],
                                         start=True, stop=True)
                    last.then_inc(S["a_proj"], 1)
                    pe.matmul(M0[:, 2 * P:3 * P], a_xct[:, P:2 * P], wt[:, WV0, :],
                              start=True, stop=True).then_inc(S["a_vproj"], 1)
                if B:
                    pe.wait_ge(S["b_xst_ready"], tb + 1)
                    pe.matmul(B0[:, :], b_xst[:, :], w_sim[:, :], start=True, stop=True).then_inc(S["b_simmm"], 1)
                    wait(pe, S["b_cg_ready"], tb)
                    for c in range(EC):
                        last = pe.matmul(H[:, c * P:(c + 1) * P], down_t[:, c, :], b_xst[:, :], start=True, stop=True)
                    last.then_inc(S["b_hid"], 1)

                def score(g):
                    if g == 0:
                        pe.wait_ge(S["a_kbd_ready"], ta + 1)
                        wait(pe, S["c_exp"], 2 * tc)
                    if g >= 2:
                        pe.wait_ge(S["a_exp"], GROUPS * ta + g - 1)
                    pe.matmul(SC[:, (g % 2) * 512:(g % 2) * 512 + 512], a_qkt[:, 0:P],
                              a_kbd[:, GROUP * g:GROUP * (g + 1), :], start=True, stop=True).then_inc(S["a_score"], 1)

                def weigh(g):
                    pe.wait_ge(S["a_exp"], GROUPS * ta + g + 1)
                    if g == 0:
                        wait(pe, S["c_ptcopy"], 2 * tc)
                    for j in range(GROUP):
                        last = pe.transpose(PT[:, j * P:(j + 1) * P], a_p[:, g % 2, j * P:(j + 1) * P], ident)
                    last.then_inc(S["a_ptr"], 1)
                    if g < 2:
                        score(g + 2)
                    pe.wait_ge(S["a_ptcopy"], GROUPS * ta + g + 1)
                    if g == 0:
                        pe.wait_ge(S["a_vready"], ta + 1)
                    for j in range(GROUP):
                        h = GROUP * g + j
                        last = pe.matmul(M1[:, h * VW:(h + 1) * VW], a_pt[:, g % 2, j * P:(j + 1) * P], a_v[:, h, :],
                                         start=True, stop=True)
                    last.then_inc(S["a_pv"], 1)

                if A:
                    score(0)
                    score(1)
                    for g in range(GROUPS):
                        weigh(g)
                    pe.wait_ge(S["a_o_ready"], ta + 1)
                    pe.transpose(M0[:, 0:P], a_o[:, :], ident).then_inc(S["a_otr"], 1)
                    pe.wait_ge(S["a_ot_ready"], ta + 1)
                    pe.matmul(M1[:, 2 * P:3 * P], a_ot[:, :], wt[:, WO0, :], start=True, stop=True)\
                        .then_inc(S["a_wo"], 1)

                def expert_head(h):
                    if h == 0:
                        pe.wait_ge(S["b_gelu"], tb + 1)
                    pe.wait_ge(S["b_w_ready"], EH * tb + h + 1)
                    for c in range(EC):
                        last = pe.matmul(H[:, c * P:(c + 1) * P], b_w[:, h % NS, c * P:(c + 1) * P], ident,
                                         start=(h == 0 and c % 4 == 0), stop=(h == EH - 1), is_transpose=True,
                                         skip_group_check=True)
                    last.then_inc(S["b_wtr"], 1)

                if B:
                    for h in range(4):
                        expert_head(h)
                if C:
                    pe.wait_ge(S["c_xn_ready"], tc + 1)
                    pe.wait_ge(S["c_ctxin"], 64 * tc + 64)
                    pe.transpose(M0[:, 0:P], c_xn[:, :], ident)
                    pe.transpose(M0[:, P:2 * P], c_ctx[:, :], ident).then_inc(S["c_tr"], 1)
                    pe.wait_ge(S["c_xct_ready"], tc + 1)
                    if A:
                        pe.wait_ge(S["x1_ready"], ta + 1)
                    pe.matmul(M1[:, 0:P], wt[:, WQ1, :], c_xct[:, 0:P], start=True, stop=True)
                    pe.matmul(M1[:, P:2 * P], wt[:, WK1, :], c_xct[:, P:2 * P], start=True, stop=True)\
                        .then_inc(S["c_qkproj"], 1)
                    pe.wait_ge(S["c_ctxc_ready"], tc + 1)
                    pe.matmul(M0[:, 0:P], c_xct[:, P:2 * P], wt[:, WV1, :], start=True, stop=True)
                    pe.matmul(M0[:, P:2 * P], c_ctxc[:, :], wt[:, WV1, :], start=True, stop=True)\
                        .then_inc(S["c_vproj"], 1)
                if B:
                    for h in range(4, EH):
                        expert_head(h)
                if C:
                    pe.wait_ge(S["c_kbd_ready"], tc + 1)
                    pe.wait_ge(S["c_qt_ready"], tc + 1)
                    for j in range(2):
                        pe.matmul(SC[:, 512 * j:512 * j + 2 * W1], c_qt[:, :], c_kbd[:, 2 * j:2 * j + 2, :],
                                  start=True, stop=True).then_inc(S["c_score"], 1)
                if B:
                    pe.wait_ge(S["b_cg_ready"], tb + 1)
                    for c in range(EC):
                        last = pe.matmul(B0[:, 0:P], b_cg[:, c * P:(c + 1) * P], up_sb[:, c, :],
                                         start=(c == 0), stop=(c == EC - 1))
                    last.then_inc(S["b_ffn"], 1)
                if C:
                    for j in range(2):
                        pe.wait_ge(S["c_exp"], 2 * tc + j + 1)
                        if j == 1:
                            pe.wait_ge(S["c_ptcopy"], 2 * tc + 1)
                        for i in range(4):
                            last = pe.transpose(PT[:, i * P:(i + 1) * P],
                                                c_p[:, 2 * j + i // 2, (i % 2) * P:(i % 2 + 1) * P], ident)
                        last.then_inc(S["c_ptr"], 1)
                        pe.wait_ge(S["c_ptcopy"], 2 * tc + j + 1)
                        if j == 0:
                            pe.wait_ge(S["c_v_ready"], tc + 1)
                        for i in range(2):
                            g = 2 * j + i
                            o = g * GROUP * VW
                            pe.matmul(M1[:, o:o + VW], c_pt[:, j, 2 * i * P:(2 * i + 1) * P], c_va[:, g, :],
                                      start=True, stop=True)
                            last = pe.matmul(M1[:, o + VW:o + GROUP * VW], c_pt[:, j, (2 * i + 1) * P:(2 * i + 2) * P],
                                             c_vb[:, g, :, :], start=True, stop=True)
                        last.then_inc(S["c_pv"], 1)
                    pe.wait_ge(S["c_o_ready"], tc + 1)
                    pe.transpose(M0[:, 0:P], c_o[:, :], ident).then_inc(S["c_otr"], 1)
                    pe.wait_ge(S["c_ot_ready"], tc + 1)
                    pe.matmul(M1[:, 2 * P:3 * P], c_ot[:, :], wt[:, WO1, :], start=True, stop=True)\
                        .then_inc(S["c_wo"], 1)
                    pe.wait_ge(S["c_yq_ready"], tc + 1)
                    pe.transpose(M0[:, 0:P], c_yq[:, :], ident).then_inc(S["c_ytr"], 1)
                    pe.wait_ge(S["c_yqt_ready"], tc + 1)
                    pe.matmul(M1[:, 0:P], c_yqt[:, :], rhs_q[:, :], start=True, stop=True).then_inc(S["c_int"], 1)
            steps(pe, step)

        @block.scalar
        def _(act):
            act.wait_ge(S["setup_pool"], 4)
            act.wait_ge(S["setup_dve"], 1)

            def copy(to, of):
                return act.activation(to, of, ACT.Copy)

            def step(s, A, B, C):
                ta, tb, tc = s, s - 1, s - 2
                if A:
                    act.wait_ge(S["a_tr"], ta + 1)
                    copy(a_xct[:, :], M0[:, 0:2 * P]).then_inc(S["a_xct_ready"], 1)
                if B:
                    act.wait_ge(S["b_tr"], tb + 1)
                    copy(b_xst[:, :], B0[:, 0:P]).then_inc(S["b_xst_ready"], 1)
                if A:
                    act.wait_ge(S["a_vproj"], ta + 1)
                    copy(a_v[:, :, 0:DK], M0[:, 2 * P:3 * P].rearrange("p (h d) -> p h d", d=DK))\
                        .then_inc(S["a_vready"], 1)
                if B:
                    act.wait_ge(S["b_simmm"], tb + 1)
                    copy(b_sim[:, :, :], B0[:, :].rearrange("p (h k) -> p h k", k=NKEY)).then_inc(S["b_sim_ready"], 1)
                    act.wait_ge(S["b_hid"], tb + 1)
                    act.activation(b_g[:, :], H[:, :], ACT.Gelu).then_inc(S["b_gelu"], 1)
                if A:
                    for g in range(GROUPS + 1):
                        if g < GROUPS:
                            act.wait_ge(S["a_max"], GROUPS * ta + g + 1)
                            for j in range(GROUP):
                                h = GROUP * g + j
                                sc = (g % 2) * 512 + j * P
                                last = act.activation(a_p[:, g % 2, j * P:(j + 1) * P], SC[:, sc:sc + P], ACT.Exp,
                                                      bias=a_nmax[:, h:h + 1])
                            last.then_inc(S["a_exp"], 1)
                        if g > 0:
                            act.wait_ge(S["a_ptr"], GROUPS * ta + g)
                            copy(a_pt[:, (g - 1) % 2, :], PT[:, :]).then_inc(S["a_ptcopy"], 1)
                    act.wait_ge(S["a_otr"], ta + 1)
                    copy(a_ot[:, :], M0[:, 0:P]).then_inc(S["a_ot_ready"], 1)
                if C:
                    act.wait_ge(S["c_tr"], tc + 1)
                    copy(c_xct[:, :], M0[:, 0:2 * P]).then_inc(S["c_xct_ready"], 1)
                    act.wait_ge(S["c_qkproj"], tc + 1)
                    act.activation(c_kt[:, :], M1[:, P:2 * P], ACT.Identity, bias=cols[:, 2:3])
                    act.activation(c_qt[:, :], M1[:, 0:P], ACT.Identity, bias=cols[:, 4:5], scale=SCALE)\
                        .then_inc(S["c_qt_ready"], 1)
                    act.wait_ge(S["c_vproj"], tc + 1)
                    va = M0[:, 0:P].rearrange("p (g c d) -> p g c d", c=GROUP, d=DK)
                    vb = M0[:, P:2 * P].rearrange("p (g c d) -> p g c d", c=GROUP, d=DK)
                    copy(c_va[:, :, 0:DK], va[:, :, 0, :])
                    for i, (p0, p1) in enumerate(((0, 64), (64, 96), (96, 128))):
                        last = copy(c_vb[p0:p1, :, i, 0:DK], vb[p0:p1, :, i + 1, :])
                    last.then_inc(S["c_v_ready"], 1)
                    act.wait_ge(S["c_max"], tc + 1)
                    for j in range(2):
                        for i in range(2):
                            g = 2 * j + i
                            for c in range(GROUP):
                                sc = 512 * j + i * W1 + OFF1[c]
                                last = act.activation(c_p[:, g, OFF1[c]:OFF1[c] + NK1[c]], SC[:, sc:sc + NK1[c]],
                                                      ACT.Exp, bias=c_nmax[:, c, g:g + 1])
                        last.then_inc(S["c_exp"], 1)
                    for j in range(2):
                        act.wait_ge(S["c_ptr"], 2 * tc + j + 1)
                        copy(c_pt[:, j, :], PT[:, :]).then_inc(S["c_ptcopy"], 1)
                    act.wait_ge(S["c_otr"], tc + 1)
                    copy(c_ot[:, :], M0[:, 0:P]).then_inc(S["c_ot_ready"], 1)
                    act.wait_ge(S["c_ytr"], tc + 1)
                    copy(c_yqt[:, :], M0[:, 0:P]).then_inc(S["c_yqt_ready"], 1)
            steps(act, step)

        @block.gpsimd
        def _(pool):
            pool.memset(neghalf[:, :], -0.5)
            pool.memset(a_v[:, :, DK:VW], 1.0)
            pool.memset(c_va[:, :, DK:VW], 1.0)
            pool.memset(c_vb[:, :, :, :], 0.0)
            pool.memset(c_p[:, :, W1:2 * P], 0.0).then_inc(S["setup_pool"], 1)
            pool.wait_ge(S["setup_pool"], 1)
            for i, (p0, p1) in enumerate(((0, 64), (64, 96), (96, 128))):
                pool.memset(c_vb[p0:p1, :, i, DK:VW], 1.0).then_inc(S["setup_pool"], 1)
                pool.wait_ge(S["setup_pool"], i + 2)
            pool.wait_ge(S["setup_dve"], 1)

            def inverse_root(var, r, aggr, eps, rstd, t):
                hold(pool, aggr, t + 1, S["pool_held"])
                pool.tensor_scalar(r[:, 1:2], var, EPS, None, ALU.add).then_inc(eps, 1)
                pool.wait_ge(eps, t + 1)
                pool.tensor_tensor(r[:, 0:1], r[:, 1:2], neghalf[:, :], ALU.pow).then_inc(rstd, 1)

            def step(s, A, B, C):
                ta, tb, tc = s, s - 1, s - 2
                if A:
                    inverse_root(a_mv[:, 1:2], a_r, S["a_aggr"], S["a_eps"], S["a_rstd"], ta)
                if B:
                    hold(pool, S["b_aggr"], tb + 1, S["pool_held"])
                    pool.tensor_scalar(b_r[:, 0:1], b_mv[:, 1:2], EPS, None, ALU.add).then_inc(S["b_p1"], 1)
                    pool.wait_ge(S["b_p1"], tb + 1)
                    pool.tensor_tensor(b_r[:, 1:2], b_r[:, 0:1], neghalf[:, :], ALU.pow).then_inc(S["b_p2"], 1)
                    hold(pool, S["b_p2"], tb + 1, S["pool_held"])
                    pool.tensor_scalar(b_r[:, 2:3], b_mv[:, 1:2], b_r[:, 1:2], b_r[:, 1:2], ALU.mult, ALU.mult)\
                        .then_inc(S["b_p3"], 1)
                    hold(pool, S["b_p3"], tb + 1, S["pool_held"])
                    pool.tensor_scalar(b_r[:, 3:4], b_r[:, 2:3], EPS, None, ALU.add).then_inc(S["b_p4"], 1)
                    pool.wait_ge(S["b_p4"], tb + 1)
                    pool.tensor_tensor(b_r[:, 4:5], b_r[:, 3:4], neghalf[:, :], ALU.pow).then_inc(S["b_p5"], 1)
                    pool.wait_ge(S["b_p5"], tb + 1)
                    pool.tensor_tensor(b_r[:, 5:6], b_r[:, 1:2], b_r[:, 4:5], ALU.mult).then_inc(S["b_p6"], 1)
                if C:
                    inverse_root(c_mv[:, 1:2], c_r, S["c_aggr"], S["c_eps"], S["c_rstd"], tc)
                if B:
                    hold(pool, S["x2_ready"], tb, S["pool_held"])
                    pool.tensor_copy(b_x1[:, :], x1[:, :]).then_inc(S["b_kept"], 1)
                if C:
                    wait(pool, S["c_x3_ready"], tc)
                    pool.tensor_tensor(c_x2[:, :], x2[:, :], attn_bias[:, :], ALU.add).then_inc(S["c_kept"], 1)
                if B:
                    pool.wait_ge(S["b_t3"], tb + 1)
                    wait(pool, S["b_c3"], tb)
                    halves = b_top[:, :, :].rearrange("p (h a) k -> p h a k", a=2)
                    at = 0
                    for i, ni, nj in PAIRS:
                        to = b_cand[:, :, at:at + ni * nj]
                        if ni == 1:
                            one = halves[:, :, 0, i:i + 1].to_broadcast([P, EH, nj])
                            two = halves[:, :, 1, 0:nj]
                        elif nj == 1:
                            one = halves[:, :, 0, i:i + ni]
                            two = halves[:, :, 1, 0:1].to_broadcast([P, EH, ni])
                        else:
                            to = to.rearrange("p h (i j) -> p h i j", j=nj)
                            one = halves[:, :, 0, i:i + ni].unsqueeze(3).to_broadcast([P, EH, ni, nj])
                            two = halves[:, :, 1, 0:nj].unsqueeze(2).to_broadcast([P, EH, ni, nj])
                        last = pool.tensor_tensor(to, one, two, ALU.add)
                        at += ni * nj
                    last.then_inc(S["b_cand_ready"], 1)
                    for h in range(EH):
                        wait(pool, S["b_w_ready"], EH * tb + h + 1 - NS)
                        pool.tensor_tensor(
                            b_sum[:, h % NS, :].rearrange("p (i j) -> p i j", j=NKEY),
                            b_sim[:, 2 * h, :].unsqueeze(2).to_broadcast([P, NKEY, NKEY]),
                            b_sim[:, 2 * h + 1, :].unsqueeze(1).to_broadcast([P, NKEY, NKEY]),
                            ALU.add).then_inc(S["b_sum_ready"], 1)
                if C:
                    hold(pool, S["c_xct_ready"], tc + 1, S["pool_held"])
                    for at, n in ((0, 64), (64, 32), (96, 16), (112, 16)):
                        last = pool.tensor_copy(c_ctxc[:, at:at + n], c_xct[:, P:P + n])
                    last.then_inc(S["c_ctxc_ready"], 1)
                    inverse_root(c_mv3[:, 1:2], c_r3, S["c_aggr3"], S["c_eps3"], S["c_rstd3"], tc)
            steps(pool, step)

        @block.vector
        def _(dve):
            dve.wait_ge(S["w_loaded"], LOADED)
            dve.tensor_scalar(cols[:, 4:5], cols[:, 1:2], SCALE, None, ALU.mult)
            dve.tensor_copy(bv_rep[:, :], cols[:, 3:4].to_broadcast([P, P])).then_inc(S["w_ready"], 1)
            banks = [M0[:, :], M1[:, :], PT[:, :], B0[:, :]]
            for r in range(ROUNDS):
                n = min(4, SLOTS - 4 * r)
                dve.wait_ge(S["tr_done"], r + 1)
                dve.tensor_copy(wt[:, 4 * r:4 * r + n, :].rearrange("p a b -> p (a b)"),
                                banks[r % 4][:, 0:n * P]).then_inc(S["tr_copied"], 1)
            dve.wait_ge(S["tr_copied"], ROUNDS)
            for i, w in enumerate((WQ0, WK0)):
                pair = wt[:, w, :].rearrange("p (n a) -> p n a", a=2)
                for a in range(2):
                    dve.tensor_copy(swapped[:, i, :].rearrange("p (n a) -> p n a", a=2)[:, :, a], pair[:, :, 1 - a])
            dve.tensor_scalar(down_t[:, :, :], wt[:, DOWN:DOWN + EC, :], cols[:, 0:1], None, ALU.mult)
            dve.tensor_reduce(rhs_amax[:, 0:1], wt[:, RHS, :], AX_X, ALU.max, apply_absolute_value=True)\
                .then_inc(S["w_ready"], 1)
            dve.wait_ge(S["w_ready"], 2)
            dve.tensor_scalar(rhs_amax[:, 1:2], rhs_amax[:, 0:1], 1e-12, 1.0 / QMAX, ALU.max, ALU.mult)\
                .then_inc(S["w_ready"], 1)
            dve.wait_ge(S["w_ready"], 3)
            dve.reciprocal(rhs_amax[:, 2:3], rhs_amax[:, 1:2]).then_inc(S["w_ready"], 1)
            dve.tensor_copy(rhs_srep[:, :], rhs_amax[:, 1:2].to_broadcast([P, P]))
            dve.wait_ge(S["w_ready"], 4)
            dve.tensor_scalar(rhs_r[:, :], wt[:, RHS, :], rhs_amax[:, 2:3], ROUND, ALU.mult, ALU.add)\
                .then_inc(S["w_ready"], 1)
            dve.wait_ge(S["w_ready"], 5)
            dve.tensor_scalar(rhs_r[:, :], rhs_r[:, :], ROUND, QMAX, ALU.subtract, ALU.min).then_inc(S["w_ready"], 1)
            dve.wait_ge(S["w_ready"], 6)
            dve.tensor_scalar(rhs_r[:, :], rhs_r[:, :], -QMAX, None, ALU.max).then_inc(S["rq_ready"], 1)
            dve.wait_ge(S["sim_done"], 1)
            dve.tensor_scalar(w_sim[:, :], SC[:, 0:512], cols[:, 0:1], None, ALU.mult)
            dve.wait_ge(S["bo_done"], 1)
            dve.tensor_tensor(attn_bias[:, :], SC[:, 512:512 + P], bo_rep[:, :], ALU.add)
            dve.wait_ge(S["rq_done"], 1)
            dve.tensor_copy(rhs_q[:, :], H[:, 0:P])
            dve.tensor_copy(rhs_row[:, :], H[:, P:2 * P]).then_inc(S["setup_dve"], 1)
            dve.wait_ge(S["setup_dve"], 1)

            def stats(src, st, mv, stat, aggr, t):
                dve.bn_stats(st[:, :], src).then_inc(stat, 1)
                hold(dve, stat, t + 1, S["dve_held"])
                dve.bn_aggr(mv[:, :], st[:, :]).then_inc(aggr, 1)

            def normalise(to, src, mv, r, rstd, done, t):
                dve.wait_ge(rstd, t + 1)
                dve.tensor_scalar(to, src, mv[:, 0:1], r, ALU.subtract, ALU.mult).then_inc(done, 1)

            def step(s, A, B, C):
                ta, tb, tc = s, s - 1, s - 2
                if A:
                    dve.wait_ge(S["a_xin"], 16 * ta + 16)
                    stats(a_x[:, :], a_st, a_mv, S["a_stat"], S["a_aggr"], ta)
                if B:
                    dve.wait_ge(S["x1_ready"], tb + 1)
                    stats(x1[:, :], b_st, b_mv, S["b_stat"], S["b_aggr"], tb)
                if C:
                    dve.wait_ge(S["x2_ready"], tc + 1)
                    stats(x2[:, :], c_st, c_mv, S["c_stat"], S["c_aggr"], tc)
                if A:
                    wait(dve, S["a_tr"], ta)
                    normalise(a_xn[:, :], a_x[:, :], a_mv, a_r[:, 0:1], S["a_rstd"], S["a_xn_ready"], ta)
                if B:
                    wait(dve, S["b_tr"], tb)
                    normalise(b_xs[:, :], x1[:, :], b_mv, b_r[:, 5:6], S["b_p6"], S["b_xs_ready"], tb)
                if C:
                    wait(dve, S["c_tr"], tc)
                    normalise(c_xn[:, :], x2[:, :], c_mv, c_r[:, 0:1], S["c_rstd"], S["c_xn_ready"], tc)
                if A:
                    dve.wait_ge(S["a_proj"], ta + 1)
                    dve.tensor_tensor(a_ropec[:, :], M1[:, 0:2 * P], cos_t, ALU.mult)
                    dve.tensor_tensor(a_ropes[:, :], M1[:, 2 * P:4 * P], sin_t, ALU.mult).then_inc(S["a_rs"], 1)
                    dve.wait_ge(S["a_rs"], ta + 1)
                    wait(dve, S["a_score"], GROUPS * ta)
                    dve.tensor_tensor(a_qkt[:, :], a_ropec[:, :], a_ropes[:, :], ALU.add).then_inc(S["a_qk_ready"], 1)
                    dve.wait_ge(S["a_qk_ready"], ta + 1)
                    dve.tensor_tensor(a_kbd[:, :, :], a_qkt[:, P:2 * P].unsqueeze(1).to_broadcast([P, HEADS, P]),
                                      hmask.unsqueeze(2).to_broadcast([P, HEADS, P]), ALU.mult)\
                        .then_inc(S["a_kbd_ready"], 1)
                if B:
                    hold(dve, S["b_sim_ready"], tb + 1, S["dve_held"])
                    for i in range(2 * EH):
                        last = dve.max(b_top[:, i, 0:8], b_sim[:, i, :])
                    last.then_inc(S["b_t1"], 1)

                def largest(g):
                    dve.wait_ge(S["a_score"], GROUPS * ta + g + 1)
                    dve.tensor_reduce(a_nmax[:, GROUP * g:GROUP * (g + 1)],
                                      SC[:, (g % 2) * 512:(g % 2) * 512 + 512].rearrange("p (h k) -> p h k", k=P),
                                      AX_X, ALU.max, negate=True).then_inc(S["a_max"], 1)
                if A:
                    largest(0)
                    largest(1)
                if B:
                    hold(dve, S["b_t1"], tb + 1, S["dve_held"])
                    for i in range(2 * EH):
                        last = dve.match_replace(b_rest[:, i, :], b_top[:, i, 0:8], b_sim[:, i, :], LOW)
                    last.then_inc(S["b_t2"], 1)
                if A:
                    largest(2)
                if B:
                    hold(dve, S["b_t2"], tb + 1, S["dve_held"])
                    for i in range(2 * EH):
                        last = dve.max(b_top[:, i, 8:16], b_rest[:, i, :])
                    last.then_inc(S["b_t3"], 1)
                if A:
                    largest(3)
                if B:
                    hold(dve, S["b_cand_ready"], tb + 1, S["dve_held"])
                    for h in range(EH):
                        last = dve.max(b_ctop[:, h, 0:8], b_cand[:, h, :])
                    last.then_inc(S["b_c1"], 1)
                    hold(dve, S["b_c1"], tb + 1, S["dve_held"])
                    for h in range(EH):
                        last = dve.match_replace(b_crest[:, h, :], b_ctop[:, h, 0:8], b_cand[:, h, :], LOW)
                    last.then_inc(S["b_c2"], 1)
                if A:
                    dve.wait_ge(S["a_pv"], GROUPS * ta + GROUPS)
                    heads = M1[:, 0:HEADS * VW].rearrange("p (h d) -> p h d", d=VW)
                    dve.reciprocal(a_rec[:, :], heads[:, :, DK]).then_inc(S["a_rec_ready"], 1)
                    dve.wait_ge(S["a_rec_ready"], ta + 1)
                    dve.tensor_tensor(a_o[:, :].rearrange("p (h d) -> p h d", d=DK), heads[:, :, 0:DK],
                                      a_rec[:, :].unsqueeze(2).to_broadcast([P, HEADS, DK]), ALU.mult)\
                        .then_inc(S["a_o_ready"], 1)
                if B:
                    hold(dve, S["b_c2"], tb + 1, S["dve_held"])
                    for h in range(EH):
                        last = dve.max(b_ctop[:, h, 8:16], b_crest[:, h, :])
                    last.then_inc(S["b_c3"], 1)
                    dve.wait_ge(S["b_c3"], tb + 1)
                    dve.tensor_scalar(b_thr[:, :], b_ctop[:, :, TOP - 1], 0.0, None, ALU.max)\
                        .then_inc(S["b_thr_ready"], 1)
                if A:
                    dve.wait_ge(S["a_wo"], ta + 1)
                    dve.wait_ge(S["a_xresin"], 16 * ta + 16)
                    if B:
                        dve.wait_ge(S["b_kept"], tb + 1)
                    dve.tensor_tensor(x1[:, :], M1[:, 2 * P:3 * P], a_xres[:, :], ALU.add).then_inc(S["x1_ready"], 1)
                if B:
                    dve.wait_ge(S["b_thr_ready"], tb + 1)

                def expert_weight(h):
                    dve.wait_ge(S["b_sum_ready"], EH * tb + h + 1)
                    wait(dve, S["b_wtr"], EH * tb + h + 1 - NS)
                    dve.scalar_tensor_tensor(b_w[:, h % NS, :], b_sum[:, h % NS, :], b_thr[:, h:h + 1],
                                             b_sum[:, h % NS, :], ALU.is_ge, ALU.mult).then_inc(S["b_w_ready"], 1)
                if B:
                    for h in range(4):
                        expert_weight(h)
                if C:
                    dve.wait_ge(S["c_qt_ready"], tc + 1)
                    wait(dve, S["c_score"], 2 * tc)
                    for c in range(GROUP):
                        n = NK1[c]
                        last = dve.tensor_tensor(
                            c_kbd[:, :, OFF1[c]:OFF1[c] + n], c_kt[:, 0:n].unsqueeze(1).to_broadcast([P, GROUPS, n]),
                            hmask[:, c:HEADS:GROUP].unsqueeze(2).to_broadcast([P, GROUPS, n]), ALU.mult)
                    last.then_inc(S["c_kbd_ready"], 1)
                if B:
                    for h in range(4, EH):
                        expert_weight(h)
                if C:
                    dve.wait_ge(S["c_score"], 2 * tc + 2)
                    sc = SC[:, :].rearrange("p (j k) -> p j k", k=512)[:, :, 0:2 * W1]\
                        .rearrange("p j (i k) -> p j i k", k=W1)
                    for c in range(GROUP):
                        last = dve.tensor_reduce(c_nmax[:, c, :].rearrange("p (j i) -> p j i", i=2),
                                                 sc[:, :, :, OFF1[c]:OFF1[c] + NK1[c]], AX_X, ALU.max, negate=True)
                    last.then_inc(S["c_max"], 1)
                if B:
                    dve.wait_ge(S["b_wtr"], EH * tb + EH)
                    wait(dve, S["b_ffn"], tb)
                    dve.tensor_tensor(b_cg[:, :], H[:, :], b_g[:, :], ALU.mult).then_inc(S["b_cg_ready"], 1)
                    dve.wait_ge(S["b_ffn"], tb + 1)
                    dve.wait_ge(S["b_kept"], tb + 1)
                    if C:
                        dve.wait_ge(S["c_kept"], tc + 1)
                    dve.tensor_tensor(x2[:, :], B0[:, 0:P], b_x1[:, :], ALU.add).then_inc(S["x2_ready"], 1)
                if C:
                    dve.wait_ge(S["c_pv"], 2 * tc + 2)
                    heads = M1[:, 0:HEADS * VW].rearrange("p (h d) -> p h d", d=VW)
                    dve.reciprocal(c_rec[:, :], heads[:, :, DK]).then_inc(S["c_rec_ready"], 1)
                    dve.wait_ge(S["c_rec_ready"], tc + 1)
                    dve.tensor_tensor(c_o[:, :].rearrange("p (h d) -> p h d", d=DK), heads[:, :, 0:DK],
                                      c_rec[:, :].unsqueeze(2).to_broadcast([P, HEADS, DK]), ALU.mult)\
                        .then_inc(S["c_o_ready"], 1)
                    dve.wait_ge(S["c_wo"], tc + 1)
                    dve.wait_ge(S["c_kept"], tc + 1)
                    dve.tensor_tensor(c_x3[:, :], M1[:, 2 * P:3 * P], c_x2[:, :], ALU.add).then_inc(S["c_x3_ready"], 1)
                    dve.wait_ge(S["c_x3_ready"], tc + 1)
                    stats(c_x3[:, :], c_st3, c_mv3, S["c_stat3"], S["c_aggr3"], tc)
                    normalise(c_y[:, :], c_x3[:, :], c_mv3, c_r3[:, 0:1], S["c_rstd3"], S["c_y_ready"], tc)
                    dve.wait_ge(S["c_y_ready"], tc + 1)
                    dve.tensor_reduce(c_s[:, 0:1], c_y[:, :], AX_X, ALU.max, apply_absolute_value=True)\
                        .then_inc(S["c_s1"], 1)
                    dve.wait_ge(S["c_s1"], tc + 1)
                    dve.tensor_scalar(c_s[:, 1:2], c_s[:, 0:1], 1e-12, 1.0 / QMAX, ALU.max, ALU.mult)\
                        .then_inc(S["c_s2"], 1)
                    dve.wait_ge(S["c_s2"], tc + 1)
                    dve.reciprocal(c_s[:, 2:3], c_s[:, 1:2]).then_inc(S["c_s3"], 1)
                    dve.wait_ge(S["c_s3"], tc + 1)
                    dve.tensor_scalar(c_yr[:, :], c_y[:, :], c_s[:, 2:3], ROUND, ALU.mult, ALU.add)\
                        .then_inc(S["c_yr_ready"], 1)
                    dve.wait_ge(S["c_yr_ready"], tc + 1)
                    dve.tensor_scalar(c_yc[:, :], c_yr[:, :], ROUND, QMAX, ALU.subtract, ALU.min)\
                        .then_inc(S["c_yc_ready"], 1)
                    dve.wait_ge(S["c_yc_ready"], tc + 1)
                    dve.tensor_scalar(c_yq[:, :], c_yc[:, :], -QMAX, None, ALU.max).then_inc(S["c_yq_ready"], 1)
                    dve.wait_ge(S["c_int"], tc + 1)
                    dve.scalar_tensor_tensor(c_d[:, :], M1[:, 0:P], c_s[:, 1:2], rhs_row[:, :], ALU.mult, ALU.mult)\
                        .then_inc(S["c_d_ready"], 1)
                    dve.wait_ge(S["c_d_ready"], tc + 1)
                    wait(dve, S["stored"], 16 * tc)
                    dve.tensor_tensor(c_out[:, :], c_d[:, :], c_x3[:, :], ALU.add).then_inc(S["c_out_ready"], 1)
            steps(dve, step)


ROUNDS = -(-SLOTS // 4)
LOADED = 19 * 16


_INS = ['x', 'ctx_1024', 'L0_xattn_W_q', 'L0_xattn_W_k', 'L0_xattn_W_v', 'L0_xattn_W_o', 'L0_ffn_norm_w', 'L0_ffn_wq',
        'L0_ffn_keys', 'L0_ffn_expert_down', 'L0_ffn_expert_up', 'L1_xattn_Wq', 'L1_xattn_bq', 'L1_xattn_Wk',
        'L1_xattn_bk', 'L1_xattn_Wv', 'L1_xattn_bv', 'L1_xattn_Wo', 'L1_xattn_bo', 'L1_ffn_rhs']


def constants():
    import numpy as np
    f = np.float32
    order = np.concatenate([np.arange(a, P, s) for a, s in ((0, 8), (4, 8), (2, 4), (1, 2))])
    inv_freq = f(1.0) / np.power(f(10000.0), np.arange(0, DK, 2, dtype=f) / f(DK)).astype(f)
    angle = np.outer(np.arange(P, dtype=f), inv_freq).astype(f)
    pair = (np.arange(P) % DK) // 2
    cos, sin = np.cos(angle).astype(f)[:, pair].T, np.sin(angle).astype(f)[:, pair].T
    sin = sin * np.where(np.arange(P) % 2 == 0, f(-1), f(1))[:, None]
    t = np.zeros((P, C_ALL), f)
    t[:, C_ID:C_ID + P] = np.eye(P, dtype=f)
    t[:, C_COS:C_COS + P], t[:, C_COS + P:C_COS + 2 * P] = cos * f(SCALE), cos[:, order]
    t[:, C_SIN:C_SIN + P], t[:, C_SIN + P:C_SIN + 2 * P] = sin * f(SCALE), sin[:, order]
    t[np.arange(P), C_MASK + np.arange(P) // DK] = 1.0
    return t


def kernel(**inputs):
    import numpy as _np
    import concourse.bacc as _bacc
    from concourse import mybir as _mybir
    from concourse.bass_utils import run_bass_kernel_spmd as _run

    nc = _bacc.Bacc("TRN2", target_bir_lowering=False, num_devices=1)
    arrays = {f"in_{n}_dram": _np.ascontiguousarray(inputs[n]) for n in _INS}
    arrays["constants_dram"] = constants()
    args = [nc.dram_tensor(n, a.shape, _mybir.dt.from_np(a.dtype), kind="ExternalInput").ap() for n, a in arrays.items()]
    shape = arrays["in_x_dram"].shape
    out = nc.dram_tensor("out_dram", shape, _mybir.dt.float32, kind="ExternalOutput").ap()
    build(nc, *args, out)
    r = _run(nc, [arrays], core_ids=[0])
    return r.results[0]["out_dram"]
```

```python
from contextlib import ExitStack

import concourse.bass as bass
from concourse import mybir

F32 = mybir.dt.float32
BF16 = mybir.dt.bfloat16
ALU = mybir.AluOpType
ACT = mybir.ActivationFunctionType
AX_X = mybir.AxisListType.X

P = 128
HEADS = 16
DK = P // HEADS
VW = DK + 1
GROUP = 4
GROUPS = HEADS // GROUP
STRIDES = (1, 2, 4, 8)
NK1 = [P // s for s in STRIDES]
OFF1 = [sum(NK1[:c]) for c in range(GROUP)]
W1 = sum(NK1)
EH = 8
NKEY = 32
TOP = 16
EXPERTS = NKEY * NKEY
EC = EXPERTS // P
PAIRS = [(0, 1, 16), (1, 1, 8), (2, 1, 5), (3, 1, 4), (4, 1, 3), (5, 3, 2), (8, 8, 1)]
NCAND = sum(a * b for _, a, b in PAIRS)
EPS = 1e-5
QMAX = 127.0
ROUND = 12582912.0
LOW = -3.0e38
SCALE = 1.0 / float(DK) ** 0.5

WQ0, WK0, WV0, WO0, WQ1, WK1, WV1, WO1 = range(8)
KEYS, SUBQ, DOWN, RHS = 8, 12, 28, 36
SLOTS = 37
C_ID, C_COS, C_SIN, C_MASK = 0, P, 3 * P, 5 * P
C_ALL = 5 * P + GROUP


def wait(eng, sem, value):
    if isinstance(value, int) and value <= 0:
        return
    eng.wait_ge(sem, value)


def hold(eng, sem, value, held):
    wait(eng, sem, value)
    eng.sem_inc(held, 1)


def build(nc, x, ctxt, wq0, wk0, wv0, wo0, norm_w, subq, keys, down, up,
          wq1, bq1, wk1, bk1, wv1, bv1, wo1, bo1, rhs, table, out):
    TILES = x.shape[0]

    with ExitStack() as stack:
        def sb(name, shape, dt=F32):
            return stack.enter_context(nc.sbuf_tensor(name, shape, dt))

        def bank(name, cols=512):
            return stack.enter_context(nc.psum_tensor(name, [P, cols], F32))

        def sem(name):
            return stack.enter_context(nc.semaphore(name))

        const = sb("const", [P, C_ALL])
        ident = const[:, C_ID:C_ID + P]
        cos_t = const[:, C_COS:C_COS + 2 * P]
        sin_t = const[:, C_SIN:C_SIN + 2 * P]
        hmask = const[:, C_MASK:C_MASK + GROUP]
        raw = sb("raw", [P, SLOTS, P])
        wt = sb("wt", [P, SLOTS, P])
        swapped = sb("swapped", [P, 2, P])
        w_sim = sb("w_sim", [P, 2 * EH * NKEY])
        down_t = sb("down_t", [P, EC, P])
        up_sb = sb("up_sb", [P, EC, P])
        cols = sb("cols", [P, 8])
        bv_rep = sb("bv_rep", [P, P])
        bo_rep = sb("bo_rep", [P, P])
        attn_bias = sb("attn_bias", [P, P])
        rhs_amax = sb("rhs_amax", [P, 4])
        rhs_r = sb("rhs_r", [P, P])
        rhs_srep = sb("rhs_srep", [P, P])
        rhs_q = sb("rhs_q", [P, P], BF16)
        rhs_row = sb("rhs_row", [P, P])
        neghalf = sb("neghalf", [P, 1])
        unused = sb("unused", [P, 1])

        a_x = sb("a_x", [P, P])
        a_xres = sb("a_xres", [P, P])
        a_ctx = sb("a_ctx", [P, P])
        a_st = sb("a_st", [P, 6])
        a_mv = sb("a_mv", [P, 2])
        a_r = sb("a_r", [P, 2])
        a_xn = sb("a_xn", [P, P])
        xct = sb("xct", [P, 4 * P])
        a_v = sb("a_v", [P, HEADS, VW])
        a_ropec = sb("a_ropec", [P, 2 * P])
        a_ropes = sb("a_ropes", [P, 2 * P])
        a_qkt = sb("a_qkt", [P, 2 * P])
        a_kbd = sb("a_kbd", [P, GROUP, P])
        a_nmax = sb("a_nmax", [P, HEADS])
        a_p = sb("a_p", [P, 2, GROUP * P])
        a_pt = sb("a_pt", [P, 2, GROUP * P])
        a_rec = sb("a_rec", [P, HEADS])
        a_o = sb("a_o", [P, P])
        a_ot = sb("a_ot", [P, P])
        x1 = sb("x1", [P, P])
        f_x1 = sb("f_x1", [P, P])
        g_x1 = sb("g_x1", [P, P])
        b_st = sb("b_st", [P, 6])
        b_mv = sb("b_mv", [P, 2])
        b_r = sb("b_r", [P, 8])
        b_xs = sb("b_xs", [P, P])
        b_xst = sb("b_xst", [P, P])
        b_g = sb("b_g", [P, EXPERTS])
        b_sim = sb("b_sim", [P, 2 * EH, NKEY])
        b_simg = sb("b_simg", [P, 2 * EH, NKEY])
        b_rest = sb("b_rest", [P, 2 * EH, NKEY])
        b_top = sb("b_top", [P, 2 * EH, TOP])
        b_cand = sb("b_cand", [P, EH, NCAND])
        b_crest = sb("b_crest", [P, EH, NCAND])
        b_ctop = sb("b_ctop", [P, EH, TOP])
        b_thr = sb("b_thr", [P, EH])
        NS = 4
        NW = 4
        b_sum = sb("b_sum", [P, NS, EXPERTS])
        b_w = sb("b_w", [P, NW, EXPERTS])
        b_cg = sb("b_cg", [P, EXPERTS])
        x2 = sb("x2", [P, P])
        c_x2 = sb("c_x2", [P, P])
        c_ctx = sb("c_ctx", [P, P])
        c_st = sb("c_st", [P, 6])
        c_mv = sb("c_mv", [P, 2])
        c_r = sb("c_r", [P, 2])
        c_xn = sb("c_xn", [P, P])
        c_ctxc = sb("c_ctxc", [P, P])
        c_qt = sb("c_qt", [P, P])
        c_kt = sb("c_kt", [P, P])
        c_va = sb("c_va", [P, GROUPS, VW])
        c_vb = sb("c_vb", [P, GROUPS, 3, VW])
        c_kbd = sb("c_kbd", [P, W1])
        c_nmax = sb("c_nmax", [P, GROUP, GROUPS])
        c_p = sb("c_p", [P, GROUPS, 2 * P])
        c_pt = sb("c_pt", [P, 2, 4 * P])
        c_rec = sb("c_rec", [P, HEADS])
        c_o = sb("c_o", [P, P])
        c_ot = sb("c_ot", [P, P])
        c_x3 = sb("c_x3", [P, P])
        d_st = sb("d_st", [P, 6])
        d_mv = sb("d_mv", [P, 2])
        d_r = sb("d_r", [P, 2])
        d_y = sb("d_y", [P, P])
        d_s = sb("d_s", [P, 3])
        d_yr = sb("d_yr", [P, P])
        d_yc = sb("d_yc", [P, P])
        d_yq = sb("d_yq", [P, P])
        d_yqt = sb("d_yqt", [P, P], BF16)
        d_d = sb("d_d", [P, P])
        d_out = sb("d_out", [P, P])

        M0 = bank("M0")
        M1 = bank("M1")
        SC = bank("SC", 1024)
        PT = bank("PT")
        H = bank("H", 1024)
        B0 = bank("B0")

        names = """w_loaded tr_done tr_copied w_ready sim_done bo_done rq_ready rq_done setup_dve setup_pool
        t_tr xct_ready
        a_xin a_xresin a_ctxin a_stat a_aggr a_eps a_rstd a_xn_ready a_proj a_vproj a_vready a_rs
        a_qk_ready a_kbd_ready a_score a_max a_exp a_ptr a_ptcopy a_pv a_rec_ready a_o_ready a_otr a_ot_ready a_wo x1_ready
        f_kept g_kept b_stat b_aggr b_p1 b_p2 b_p3 b_p4 b_p5 b_p6 b_xs_ready b_tr b_xst_ready b_simmm b_sim_ready
        b_simg_ready b_t1 b_t2 b_t3 b_cand_ready b_c1 b_c2 b_c3 b_thr_ready
        b_hid b_gelu b_sum_ready b_w_ready b_wtr b_cg_ready b_ffn x2_ready
        c_ctxin c_kept c_stat c_aggr c_eps c_rstd c_xn_ready c_ctxc_ready c_qkproj c_vproj c_qt_ready
        c_v_ready c_kbd_ready c_score c_max c_exp c_ptr c_ptcopy c_pv c_rec_ready c_o_ready c_otr c_ot_ready c_wo x3_ready
        d_stat d_aggr d_eps d_rstd d_y_ready d_s1 d_s2 d_s3 d_yr_ready d_yc_ready d_yq_ready d_ytr
        d_yqt_ready d_int d_d_ready d_out_ready stored dve_held pool_held""".split()
        S = {n: sem(n) for n in names}

        block = stack.enter_context(nc.Block())

        def steps(eng, step):
            for s in range(5):
                step(s, True, s >= 1, s >= 2, s >= 3, s >= 4)
            with eng.Fori(5, TILES) as s:
                step(s, True, True, True, True, True)
            for s in range(TILES, TILES + 4):
                step(s, False, s < TILES + 1, s < TILES + 2, s < TILES + 3, True)

        @block.sync
        def _(sp):
            weights = [(raw[:, WQ0 + i, :], w) for i, w in enumerate((wq0, wk0, wv0, wo0, wq1, wk1, wv1, wo1))]
            weights += [
                (const[:, :], table),
                (raw[:, KEYS:KEYS + 4, :], keys.rearrange("h k p d -> (h k p) d").rearrange("(c r) d -> r c d", r=P)),
                (raw[:, SUBQ:SUBQ + 16, :], subq.rearrange("i (c d) -> i c d", d=P)),
                (raw[:, DOWN:DOWN + EC, :], down.rearrange("(c r) d -> r c d", r=P)),
                (up_sb[:, :, :], up.rearrange("(c r) d -> r c d", r=P)),
                (raw[:, RHS, :], rhs),
                (cols[:, 0:1], norm_w.rearrange("(p a) -> p a", a=1)),
                (cols[:, 1:2], bq1.rearrange("(p a) -> p a", a=1)),
                (cols[:, 2:3], bk1.rearrange("(p a) -> p a", a=1)),
                (cols[:, 3:4], bv1.rearrange("(p a) -> p a", a=1)),
                (bo_rep[:, :], bo1.rearrange("(a n) -> a n", a=1).to_broadcast([P, P])),
            ]
            for to, of in weights:
                sp.dma_start(to, of).then_inc(S["w_loaded"], 16)
            assert len(weights) * 16 == LOADED

            def load_ctx(to, t, arrived):
                for at, first, stride in ((0, 0, 8), (16, 4, 8), (32, 2, 4), (64, 1, 2)):
                    n = P // stride
                    sp.dma_start(to[at:at + n, :],
                                 ctxt[t, :, :].rearrange("(n s) d -> s n d", s=stride)[first]).then_inc(arrived, 16)

            def step(s, A, F, G, C, D):
                ta, tc, td = s, s - 3, s - 4
                if A:
                    wait(sp, S["a_xn_ready"], ta)
                    sp.dma_start(a_x[:, :], x[ta, :, :]).then_inc(S["a_xin"], 16)
                    wait(sp, S["t_tr"], s)
                    load_ctx(a_ctx, ta, S["a_ctxin"])
                if C:
                    wait(sp, S["t_tr"], s)
                    load_ctx(c_ctx, tc, S["c_ctxin"])
                if A:
                    wait(sp, S["x1_ready"], ta)
                    sp.dma_start(a_xres[:, :], x[ta, :, :]).then_inc(S["a_xresin"], 16)
                if D:
                    sp.wait_ge(S["d_out_ready"], td + 1)
                    sp.dma_start(out[td, :, :], d_out[:, :]).then_inc(S["stored"], 16)
            steps(sp, step)
            sp.wait_ge(S["stored"], 16 * TILES)

        @block.tensor
        def _(pe):
            pe.wait_ge(S["w_loaded"], LOADED)
            banks = [M0[:, :], M1[:, :], PT[:, :], B0[:, :]]
            for r in range(ROUNDS):
                wait(pe, S["tr_copied"], r - 3)
                n = min(4, SLOTS - 4 * r)
                for j in range(n):
                    last = pe.transpose(banks[r % 4][:, j * P:(j + 1) * P], raw[:, 4 * r + j, :], ident)
                last.then_inc(S["tr_done"], 1)
            pe.wait_ge(S["tr_copied"], ROUNDS)
            for hp in range(2 * EH):
                h, half = hp // 2, hp % 2
                k0 = (h % 2) * 2 * NKEY + half
                last = pe.matmul(SC[:, hp * NKEY:(hp + 1) * NKEY], wt[:, SUBQ + hp, :],
                                 wt[:, KEYS + h // 2, k0:k0 + 2 * NKEY - 1:2], start=True, stop=True)
            last.then_inc(S["sim_done"], 1)
            pe.wait_ge(S["w_ready"], 1)
            pe.matmul(SC[:, 512:512 + P], bv_rep[:, :], wt[:, WO1, :], start=True, stop=True).then_inc(S["bo_done"], 1)
            pe.wait_ge(S["rq_ready"], 1)
            pe.transpose(H[:, 0:P], rhs_r[:, :], ident)
            pe.transpose(H[:, P:2 * P], rhs_srep[:, :], ident).then_inc(S["rq_done"], 1)
            pe.wait_ge(S["setup_dve"], 1)
            pe.wait_ge(S["setup_pool"], 4)

            def step(s, A, F, G, C, D):
                ta, tf, tg, tc, td = s, s - 1, s - 2, s - 3, s - 4
                def expert_head(h, half):
                    if h == 0:
                        pe.wait_ge(S["b_gelu"], 2 * tg + half + 1)
                    pe.wait_ge(S["b_w_ready"], EH * tg + h + 1)
                    for c in range(EC // 2 * half, EC // 2 * (half + 1)):
                        last = pe.matmul(H[:, c * P:(c + 1) * P], b_w[:, h % NW, c * P:(c + 1) * P], ident,
                                         start=(h == 0 and c % 4 == 0), stop=(h == EH - 1), is_transpose=True,
                                         skip_group_check=True)
                    last.then_inc(S["b_wtr"], 1)

                def hid(half):
                    wait(pe, S["b_cg_ready"], 2 * tg - 1 + half)
                    for c in range(EC // 2 * half, EC // 2 * (half + 1)):
                        last = pe.matmul(H[:, c * P:(c + 1) * P], down_t[:, c, :], b_xst[:, :], start=True, stop=True)
                    last.then_inc(S["b_hid"], 1)

                def score(g):
                    if g == 0:
                        pe.wait_ge(S["a_kbd_ready"], ta + 1)
                        wait(pe, S["c_exp"], 2 * tc)
                    if g >= 2:
                        pe.wait_ge(S["a_exp"], GROUPS * ta + g - 1)
                    pe.matmul(SC[:, (g % 2) * 512:(g % 2) * 512 + 512], a_qkt[32 * g:32 * g + 32, 0:P],
                              a_kbd[32 * g:32 * g + 32, :, :], start=True, stop=True).then_inc(S["a_score"], 1)

                def weights(g):
                    pe.wait_ge(S["a_exp"], GROUPS * ta + g + 1)
                    if g:
                        pe.wait_ge(S["a_ptcopy"], GROUPS * ta + g)
                    else:
                        wait(pe, S["c_ptcopy"], 2 * tc)
                    for j in range(GROUP):
                        last = pe.transpose(PT[:, j * P:(j + 1) * P], a_p[:, g % 2, j * P:(j + 1) * P], ident)
                    last.then_inc(S["a_ptr"], 1)

                def weigh(g):
                    pe.wait_ge(S["a_ptcopy"], GROUPS * ta + g + 1)
                    if g == 0:
                        pe.wait_ge(S["a_vready"], ta + 1)
                    for j in range(GROUP):
                        h = GROUP * g + j
                        last = pe.matmul(M1[:, h * VW:(h + 1) * VW], a_pt[:, g % 2, j * P:(j + 1) * P], a_v[:, h, :],
                                         start=True, stop=True)
                    last.then_inc(S["a_pv"], 1)

                def ffn(half):
                    pe.wait_ge(S["b_cg_ready"], 2 * tg + half + 1)
                    if half == 0:
                        if C:
                            pe.wait_ge(S["c_qt_ready"], tc + 1)
                        if F:
                            pe.wait_ge(S["b_sim_ready"], tf + 1)
                    for c in range(EC // 2 * half, EC // 2 * (half + 1)):
                        last = pe.matmul(B0[:, 0:P], b_cg[:, c * P:(c + 1) * P], up_sb[:, c, :],
                                         start=(c == 0), stop=(c == EC - 1))
                    last.then_inc(S["b_ffn"], 1)

                def score1(g):
                    if g == 0:
                        pe.wait_ge(S["c_kbd_ready"], tc + 1)
                    if g >= 2:
                        pe.wait_ge(S["c_score"], GROUPS * tc + g - 1)
                    elif A:
                        pe.wait_ge(S["a_exp"], GROUPS * ta + 3 + g)
                    sc = 512 * (g % 2) + W1 * (g // 2)
                    pe.matmul(SC[:, sc:sc + W1], c_qt[32 * g:32 * g + 32, :], c_kbd[32 * g:32 * g + 32, :],
                              start=True, stop=True).then_inc(S["c_score"], 1)

                def weights1(j):
                    pe.wait_ge(S["c_exp"], 2 * tc + j + 1)
                    if j:
                        pe.wait_ge(S["c_ptcopy"], 2 * tc + j)
                    elif A:
                        pe.wait_ge(S["a_ptcopy"], GROUPS * ta + GROUPS)
                    for i in range(4):
                        last = pe.transpose(PT[:, i * P:(i + 1) * P],
                                            c_p[:, 2 * j + i // 2, (i % 2) * P:(i % 2 + 1) * P], ident)
                    last.then_inc(S["c_ptr"], 1)

                def weigh1(j):
                    pe.wait_ge(S["c_ptcopy"], 2 * tc + j + 1)
                    if j == 0:
                        pe.wait_ge(S["c_v_ready"], tc + 1)
                        if A:
                            pe.wait_ge(S["x1_ready"], ta + 1)
                    for i in range(2):
                        g = 2 * j + i
                        o = g * GROUP * VW
                        pe.matmul(M1[:, o:o + VW], c_pt[:, j, 2 * i * P:(2 * i + 1) * P], c_va[:, g, :],
                                  start=True, stop=True)
                        last = pe.matmul(M1[:, o + VW:o + GROUP * VW], c_pt[:, j, (2 * i + 1) * P:(2 * i + 2) * P],
                                         c_vb[:, g, :, :], start=True, stop=True)
                    last.then_inc(S["c_pv"], 1)

                if G:
                    hid(0)
                    hid(1)
                    expert_head(0, 0)
                if A or C:
                    wait(pe, S["d_d_ready"], td)
                    if A:
                        pe.wait_ge(S["a_xn_ready"], ta + 1)
                        pe.wait_ge(S["a_ctxin"], 64 * ta + 64)
                        pe.transpose(M0[:, 0:P], a_xn[:, :], ident)
                        last = pe.transpose(M0[:, P:2 * P], a_ctx[:, :], ident)
                    if C:
                        pe.wait_ge(S["c_xn_ready"], tc + 1)
                        pe.wait_ge(S["c_ctxin"], 64 * tc + 64)
                        pe.transpose(M0[:, 2 * P:3 * P], c_xn[:, :], ident)
                        last = pe.transpose(M0[:, 3 * P:4 * P], c_ctx[:, :], ident)
                    last.then_inc(S["t_tr"], 1)
                if G:
                    expert_head(0, 1)
                    expert_head(1, 0)
                if A:
                    pe.wait_ge(S["xct_ready"], s + 1)
                    wait(pe, S["x3_ready"], tc)
                    for i, w in enumerate((wt[:, WQ0, :], wt[:, WK0, :], swapped[:, 0, :], swapped[:, 1, :])):
                        last = pe.matmul(M1[:, i * P:(i + 1) * P], w, xct[:, (i % 2) * P:(i % 2 + 1) * P],
                                         start=True, stop=True)
                    last.then_inc(S["a_proj"], 1)
                    if C:
                        pe.wait_ge(S["c_ctxc_ready"], tc + 1)
                    pe.matmul(M0[:, 0:P], xct[:, P:2 * P], wt[:, WV0, :], start=True, stop=True)\
                        .then_inc(S["a_vproj"], 1)
                if G:
                    expert_head(1, 1)
                if F:
                    pe.wait_ge(S["b_xs_ready"], tf + 1)
                    wait(pe, S["x2_ready"], tg)
                    pe.transpose(B0[:, 0:P], b_xs[:, :], ident).then_inc(S["b_tr"], 1)
                if C:
                    pe.wait_ge(S["xct_ready"], s + 1)
                    pe.wait_ge(S["c_ctxc_ready"], tc + 1)
                    pe.matmul(M0[:, P:2 * P], xct[:, 3 * P:4 * P], wt[:, WV1, :], start=True, stop=True)
                    pe.matmul(M0[:, 2 * P:3 * P], c_ctxc[:, :], wt[:, WV1, :], start=True, stop=True)\
                        .then_inc(S["c_vproj"], 1)
                if F:
                    pe.wait_ge(S["b_xst_ready"], tf + 1)
                    pe.matmul(B0[:, :], b_xst[:, :], w_sim[:, :], start=True, stop=True).then_inc(S["b_simmm"], 1)
                if A:
                    score(0)
                    score(1)
                if C:
                    if F:
                        pe.wait_ge(S["b_sim_ready"], tf + 1)
                    elif G:
                        pe.wait_ge(S["x2_ready"], tg)
                    pe.matmul(B0[:, 0:P], wt[:, WQ1, :], xct[:, 2 * P:3 * P], start=True, stop=True)
                    pe.matmul(B0[:, P:2 * P], wt[:, WK1, :], xct[:, 3 * P:4 * P], start=True, stop=True)\
                        .then_inc(S["c_qkproj"], 1)
                if G:
                    expert_head(2, 0)
                    expert_head(2, 1)
                if A:
                    score(2)
                if D:
                    pe.wait_ge(S["d_yq_ready"], td + 1)
                    if A:
                        pe.wait_ge(S["a_vready"], ta + 1)
                    if C:
                        pe.wait_ge(S["c_v_ready"], tc + 1)
                    pe.transpose(M0[:, 0:P], d_yq[:, :], ident).then_inc(S["d_ytr"], 1)
                    pe.wait_ge(S["d_yqt_ready"], td + 1)
                    pe.matmul(M0[:, P:2 * P], d_yqt[:, :], rhs_q[:, :], start=True, stop=True).then_inc(S["d_int"], 1)
                if A:
                    weights(0)
                    score(3)
                    weights(1)
                if G:
                    expert_head(3, 0)
                    expert_head(3, 1)
                if A:
                    weigh(0)
                if C:
                    score1(0)
                if A:
                    weights(2)
                if C:
                    score1(1)
                    score1(2)
                if G:
                    expert_head(4, 0)
                if C:
                    score1(3)
                if G:
                    expert_head(4, 1)
                    expert_head(5, 0)
                if A:
                    weigh(1)
                    weights(3)
                    weigh(2)
                if G:
                    expert_head(5, 1)
                    expert_head(6, 0)
                if C:
                    weights1(0)
                if G:
                    expert_head(6, 1)
                if A:
                    weigh(3)
                if G:
                    expert_head(7, 0)
                    expert_head(7, 1)
                if A:
                    pe.wait_ge(S["a_o_ready"], ta + 1)
                    if D:
                        pe.wait_ge(S["d_d_ready"], td + 1)
                    pe.transpose(M0[:, 0:P], a_o[:, :], ident).then_inc(S["a_otr"], 1)
                if C:
                    weights1(1)
                if A:
                    pe.wait_ge(S["a_ot_ready"], ta + 1)
                    pe.matmul(M1[:, 2 * P:3 * P], a_ot[:, :], wt[:, WO0, :], start=True, stop=True)\
                        .then_inc(S["a_wo"], 1)
                if G:
                    ffn(0)
                if C:
                    weigh1(0)
                    weigh1(1)
                if G:
                    ffn(1)
                if C:
                    pe.wait_ge(S["c_o_ready"], tc + 1)
                    if D:
                        pe.wait_ge(S["d_d_ready"], td + 1)
                    pe.transpose(M0[:, 0:P], c_o[:, :], ident).then_inc(S["c_otr"], 1)
                    pe.wait_ge(S["c_ot_ready"], tc + 1)
                    pe.matmul(M1[:, 2 * P:3 * P], c_ot[:, :], wt[:, WO1, :], start=True, stop=True)\
                        .then_inc(S["c_wo"], 1)
            steps(pe, step)

        @block.scalar
        def _(act):
            act.wait_ge(S["setup_pool"], 4)
            act.wait_ge(S["setup_dve"], 1)

            def copy(to, of):
                return act.activation(to, of, ACT.Copy)

            def step(s, A, F, G, C, D):
                ta, tf, tg, tc, td = s, s - 1, s - 2, s - 3, s - 4
                def exps(g):
                    act.wait_ge(S["a_max"], GROUPS * ta + g + 1)
                    for j in range(GROUP):
                        h = GROUP * g + j
                        sc = (g % 2) * 512 + j * P
                        last = act.activation(a_p[:, g % 2, j * P:(j + 1) * P], SC[:, sc:sc + P], ACT.Exp,
                                              bias=a_nmax[:, h:h + 1])
                    last.then_inc(S["a_exp"], 1)

                def take(g):
                    act.wait_ge(S["a_ptr"], GROUPS * ta + g + 1)
                    copy(a_pt[:, g % 2, :], PT[:, :]).then_inc(S["a_ptcopy"], 1)

                def exps1(j):
                    if j == 0:
                        act.wait_ge(S["c_max"], tc + 1)
                    for i in range(2):
                        g = 2 * j + i
                        for c in range(GROUP):
                            sc = 512 * i + j * W1 + OFF1[c]
                            last = act.activation(c_p[:, g, OFF1[c]:OFF1[c] + NK1[c]], SC[:, sc:sc + NK1[c]],
                                                  ACT.Exp, bias=c_nmax[:, c, g:g + 1])
                    last.then_inc(S["c_exp"], 1)

                def take1(j):
                    act.wait_ge(S["c_ptr"], 2 * tc + j + 1)
                    copy(c_pt[:, j, :], PT[:, :]).then_inc(S["c_ptcopy"], 1)

                if G:
                    wait(act, S["x2_ready"], tg)
                    copy(g_x1[:, :], f_x1[:, :]).then_inc(S["g_kept"], 1)
                    for half in range(2):
                        act.wait_ge(S["b_hid"], 2 * tg + half + 1)
                        act.activation(b_g[:, half * 512:half * 512 + 512], H[:, half * 512:half * 512 + 512], ACT.Gelu)\
                            .then_inc(S["b_gelu"], 1)
                    act.activation(unused[:, :], neghalf[:, :], ACT.Exp)
                if A or C:
                    act.wait_ge(S["t_tr"], s + 1)
                    if A:
                        wait(act, S["a_vproj"], ta)
                    if C:
                        wait(act, S["c_qkproj"], tc)
                    lo, hi = (0 if A else 2 * P), (4 * P if C else 2 * P)
                    copy(xct[:, lo:hi], M0[:, lo:hi]).then_inc(S["xct_ready"], 1)
                if C:
                    for at, n in ((0, 64), (64, 32), (96, 32)):
                        last = copy(c_ctxc[:, at:at + n], M0[:, 3 * P:3 * P + n])
                    last.then_inc(S["c_ctxc_ready"], 1)
                if F:
                    act.wait_ge(S["b_tr"], tf + 1)
                    copy(b_xst[:, :], B0[:, 0:P]).then_inc(S["b_xst_ready"], 1)
                if C:
                    act.wait_ge(S["c_vproj"], tc + 1)
                    va = M0[:, P:2 * P].rearrange("p (g c d) -> p g c d", c=GROUP, d=DK)
                    vb = M0[:, 2 * P:3 * P].rearrange("p (g c d) -> p g c d", c=GROUP, d=DK)
                    copy(c_va[:, :, 0:DK], va[:, :, 0, :])
                    for i, (p0, p1) in enumerate(((0, 64), (64, 96), (96, 128))):
                        last = copy(c_vb[p0:p1, :, i, 0:DK], vb[p0:p1, :, i + 1, :])
                    last.then_inc(S["c_v_ready"], 1)
                if F:
                    act.wait_ge(S["x1_ready"], tf + 1)
                    if G:
                        act.wait_ge(S["g_kept"], tg + 1)
                    copy(f_x1[:, :], x1[:, :]).then_inc(S["f_kept"], 1)
                if A:
                    act.wait_ge(S["a_vproj"], ta + 1)
                    if C:
                        act.wait_ge(S["c_vproj"], tc + 1)
                    copy(a_v[:, :, 0:DK], M0[:, 0:P].rearrange("p (h d) -> p h d", d=DK)).then_inc(S["a_vready"], 1)
                if F:
                    act.wait_ge(S["b_simmm"], tf + 1)
                    wait(act, S["b_t2"], tf)
                    copy(b_sim[:, :, :], B0[:, :].rearrange("p (h k) -> p h k", k=NKEY)).then_inc(S["b_sim_ready"], 1)
                if A:
                    exps(0)
                    exps(1)
                if D:
                    act.wait_ge(S["d_ytr"], td + 1)
                    copy(d_yqt[:, :], M0[:, 0:P]).then_inc(S["d_yqt_ready"], 1)
                if C:
                    act.wait_ge(S["c_qkproj"], tc + 1)
                    act.activation(c_kt[:, :], B0[:, P:2 * P], ACT.Identity, bias=cols[:, 2:3])
                    act.activation(c_qt[:, :], B0[:, 0:P], ACT.Identity, bias=cols[:, 4:5], scale=SCALE)\
                        .then_inc(S["c_qt_ready"], 1)
                if A:
                    take(0)
                if F:
                    act.wait_ge(S["b_sim_ready"], tf + 1)
                    wait(act, S["b_sum_ready"], EH * tf)
                    copy(b_simg[:, :, :], b_sim[:, :, :]).then_inc(S["b_simg_ready"], 1)
                if A:
                    exps(2)
                    take(1)
                    exps(3)
                    take(2)
                if C:
                    exps1(0)
                if A:
                    take(3)
                if C:
                    exps1(1)
                    take1(0)
                if A:
                    act.wait_ge(S["a_otr"], ta + 1)
                    copy(a_ot[:, :], M0[:, 0:P]).then_inc(S["a_ot_ready"], 1)
                if C:
                    take1(1)
                    act.wait_ge(S["c_otr"], tc + 1)
                    copy(c_ot[:, :], M0[:, 0:P]).then_inc(S["c_ot_ready"], 1)
            steps(act, step)

        @block.gpsimd
        def _(pool):
            pool.memset(neghalf[:, :], -0.5)
            pool.memset(a_v[:, :, DK:VW], 1.0)
            pool.memset(c_va[:, :, DK:VW], 1.0)
            pool.memset(c_vb[:, :, :, :], 0.0)
            pool.memset(c_p[:, :, W1:2 * P], 0.0).then_inc(S["setup_pool"], 1)
            pool.wait_ge(S["setup_pool"], 1)
            for i, (p0, p1) in enumerate(((0, 64), (64, 96), (96, 128))):
                pool.memset(c_vb[p0:p1, :, i, DK:VW], 1.0).then_inc(S["setup_pool"], 1)
                pool.wait_ge(S["setup_pool"], i + 2)
            pool.wait_ge(S["setup_dve"], 1)

            def inverse_root(var, r, aggr, eps, rstd, t):
                hold(pool, aggr, t + 1, S["pool_held"])
                pool.tensor_scalar(r[:, 1:2], var, EPS, None, ALU.add).then_inc(eps, 1)
                pool.wait_ge(eps, t + 1)
                pool.tensor_tensor(r[:, 0:1], r[:, 1:2], neghalf[:, :], ALU.pow).then_inc(rstd, 1)

            def pair_sums(t, h):
                if h == 0:
                    pool.wait_ge(S["b_simg_ready"], t + 1)
                wait(pool, S["b_w_ready"], EH * t + h + 1 - NS)
                pool.tensor_tensor(
                    b_sum[:, h % NS, :].rearrange("p (i j) -> p i j", j=NKEY),
                    b_simg[:, 2 * h, :].unsqueeze(2).to_broadcast([P, NKEY, NKEY]),
                    b_simg[:, 2 * h + 1, :].unsqueeze(1).to_broadcast([P, NKEY, NKEY]),
                    ALU.add).then_inc(S["b_sum_ready"], 1)

            def step(s, A, F, G, C, D):
                ta, tf, tg, tc, td = s, s - 1, s - 2, s - 3, s - 4
                if A:
                    inverse_root(a_mv[:, 1:2], a_r, S["a_aggr"], S["a_eps"], S["a_rstd"], ta)
                if C:
                    inverse_root(c_mv[:, 1:2], c_r, S["c_aggr"], S["c_eps"], S["c_rstd"], tc)
                if F:
                    hold(pool, S["b_aggr"], tf + 1, S["pool_held"])
                    pool.tensor_scalar(b_r[:, 0:1], b_mv[:, 1:2], EPS, None, ALU.add).then_inc(S["b_p1"], 1)
                if D:
                    inverse_root(d_mv[:, 1:2], d_r, S["d_aggr"], S["d_eps"], S["d_rstd"], td)
                if F:
                    pool.wait_ge(S["b_p1"], tf + 1)
                    pool.tensor_tensor(b_r[:, 1:2], b_r[:, 0:1], neghalf[:, :], ALU.pow).then_inc(S["b_p2"], 1)
                    hold(pool, S["b_p2"], tf + 1, S["pool_held"])
                    pool.tensor_scalar(b_r[:, 2:3], b_mv[:, 1:2], b_r[:, 1:2], b_r[:, 1:2], ALU.mult, ALU.mult)\
                        .then_inc(S["b_p3"], 1)
                    hold(pool, S["b_p3"], tf + 1, S["pool_held"])
                    pool.tensor_scalar(b_r[:, 3:4], b_r[:, 2:3], EPS, None, ALU.add).then_inc(S["b_p4"], 1)
                    pool.wait_ge(S["b_p4"], tf + 1)
                    pool.tensor_tensor(b_r[:, 4:5], b_r[:, 3:4], neghalf[:, :], ALU.pow).then_inc(S["b_p5"], 1)
                    pool.wait_ge(S["b_p5"], tf + 1)
                    pool.tensor_tensor(b_r[:, 5:6], b_r[:, 1:2], b_r[:, 4:5], ALU.mult).then_inc(S["b_p6"], 1)
                if G:
                    pair_sums(tg, 4)
                    pair_sums(tg, 5)
                    pair_sums(tg, 6)
                if C:
                    wait(pool, S["x3_ready"], tc)
                    pool.tensor_tensor(c_x2[:, :], x2[:, :], attn_bias[:, :], ALU.add).then_inc(S["c_kept"], 1)
                if G:
                    pair_sums(tg, 7)
                if F:
                    pair_sums(tf, 0)
                    pair_sums(tf, 1)
                    pool.wait_ge(S["b_t3"], tf + 1)
                    wait(pool, S["b_c2"], tf)
                    halves = b_top[:, :, :].rearrange("p (h a) k -> p h a k", a=2)
                    at = 0
                    for i, ni, nj in PAIRS:
                        to = b_cand[:, :, at:at + ni * nj]
                        if ni == 1:
                            one = halves[:, :, 0, i:i + 1].to_broadcast([P, EH, nj])
                            two = halves[:, :, 1, 0:nj]
                        elif nj == 1:
                            one = halves[:, :, 0, i:i + ni]
                            two = halves[:, :, 1, 0:1].to_broadcast([P, EH, ni])
                        else:
                            to = to.rearrange("p h (i j) -> p h i j", j=nj)
                            one = halves[:, :, 0, i:i + ni].unsqueeze(3).to_broadcast([P, EH, ni, nj])
                            two = halves[:, :, 1, 0:nj].unsqueeze(2).to_broadcast([P, EH, ni, nj])
                        last = pool.tensor_tensor(to, one, two, ALU.add)
                        at += ni * nj
                    last.then_inc(S["b_cand_ready"], 1)
                    pair_sums(tf, 2)
                    pair_sums(tf, 3)
            steps(pool, step)

        @block.vector
        def _(dve):
            dve.wait_ge(S["w_loaded"], LOADED)
            dve.tensor_scalar(cols[:, 4:5], cols[:, 1:2], SCALE, None, ALU.mult)
            dve.tensor_copy(bv_rep[:, :], cols[:, 3:4].to_broadcast([P, P])).then_inc(S["w_ready"], 1)
            banks = [M0[:, :], M1[:, :], PT[:, :], B0[:, :]]
            for r in range(ROUNDS):
                n = min(4, SLOTS - 4 * r)
                dve.wait_ge(S["tr_done"], r + 1)
                dve.tensor_copy(wt[:, 4 * r:4 * r + n, :].rearrange("p a b -> p (a b)"),
                                banks[r % 4][:, 0:n * P]).then_inc(S["tr_copied"], 1)
            dve.wait_ge(S["tr_copied"], ROUNDS)
            for i, w in enumerate((WQ0, WK0)):
                pair = wt[:, w, :].rearrange("p (n a) -> p n a", a=2)
                for a in range(2):
                    dve.tensor_copy(swapped[:, i, :].rearrange("p (n a) -> p n a", a=2)[:, :, a], pair[:, :, 1 - a])
            dve.tensor_scalar(down_t[:, :, :], wt[:, DOWN:DOWN + EC, :], cols[:, 0:1], None, ALU.mult)
            dve.tensor_reduce(rhs_amax[:, 0:1], wt[:, RHS, :], AX_X, ALU.max, apply_absolute_value=True)\
                .then_inc(S["w_ready"], 1)
            dve.wait_ge(S["w_ready"], 2)
            dve.tensor_scalar(rhs_amax[:, 1:2], rhs_amax[:, 0:1], 1e-12, 1.0 / QMAX, ALU.max, ALU.mult)\
                .then_inc(S["w_ready"], 1)
            dve.wait_ge(S["w_ready"], 3)
            dve.reciprocal(rhs_amax[:, 2:3], rhs_amax[:, 1:2]).then_inc(S["w_ready"], 1)
            dve.tensor_copy(rhs_srep[:, :], rhs_amax[:, 1:2].to_broadcast([P, P]))
            dve.wait_ge(S["w_ready"], 4)
            dve.tensor_scalar(rhs_r[:, :], wt[:, RHS, :], rhs_amax[:, 2:3], ROUND, ALU.mult, ALU.add)\
                .then_inc(S["w_ready"], 1)
            dve.wait_ge(S["w_ready"], 5)
            dve.tensor_scalar(rhs_r[:, :], rhs_r[:, :], ROUND, QMAX, ALU.subtract, ALU.min).then_inc(S["w_ready"], 1)
            dve.wait_ge(S["w_ready"], 6)
            dve.tensor_scalar(rhs_r[:, :], rhs_r[:, :], -QMAX, None, ALU.max).then_inc(S["rq_ready"], 1)
            dve.wait_ge(S["sim_done"], 1)
            dve.tensor_scalar(w_sim[:, :], SC[:, 0:512], cols[:, 0:1], None, ALU.mult)
            dve.wait_ge(S["bo_done"], 1)
            dve.tensor_tensor(attn_bias[:, :], SC[:, 512:512 + P], bo_rep[:, :], ALU.add)
            dve.wait_ge(S["rq_done"], 1)
            dve.tensor_copy(rhs_q[:, :], H[:, 0:P])
            dve.tensor_copy(rhs_row[:, :], H[:, P:2 * P]).then_inc(S["setup_dve"], 1)
            dve.wait_ge(S["setup_dve"], 1)

            def stats(src, st, mv, stat, aggr, t):
                dve.bn_stats(st[:, :], src).then_inc(stat, 1)
                hold(dve, stat, t + 1, S["dve_held"])
                dve.bn_aggr(mv[:, :], st[:, :]).then_inc(aggr, 1)

            def normalise(to, src, mv, r, rstd, done, t):
                dve.wait_ge(rstd, t + 1)
                dve.tensor_scalar(to, src, mv[:, 0:1], r, ALU.subtract, ALU.mult).then_inc(done, 1)

            def step(s, A, F, G, C, D):
                ta, tf, tg, tc, td = s, s - 1, s - 2, s - 3, s - 4
                def expert_weights(h):
                    dve.wait_ge(S["b_sum_ready"], EH * tg + h + 1)
                    wait(dve, S["b_wtr"], 2 * (EH * tg + h + 1 - NW))
                    dve.scalar_tensor_tensor(b_w[:, h % NW, :], b_sum[:, h % NS, :], b_thr[:, h:h + 1],
                                             b_sum[:, h % NS, :], ALU.is_ge, ALU.mult).then_inc(S["b_w_ready"], 1)

                def weighted(half):
                    dve.wait_ge(S["b_wtr"], 2 * (EH * tg + EH) - 1 + half)
                    wait(dve, S["b_ffn"], 2 * tg - 1 + half)
                    lo, hi = half * 512, half * 512 + 512
                    dve.tensor_tensor(b_cg[:, lo:hi], H[:, lo:hi], b_g[:, lo:hi], ALU.mult).then_inc(S["b_cg_ready"], 1)

                def largest(g):
                    dve.wait_ge(S["a_score"], GROUPS * ta + g + 1)
                    dve.tensor_reduce(a_nmax[:, GROUP * g:GROUP * (g + 1)],
                                      SC[:, (g % 2) * 512:(g % 2) * 512 + 512].rearrange("p (h k) -> p h k", k=P),
                                      AX_X, ALU.max, negate=True).then_inc(S["a_max"], 1)

                if A:
                    dve.wait_ge(S["a_xin"], 16 * ta + 16)
                    stats(a_x[:, :], a_st, a_mv, S["a_stat"], S["a_aggr"], ta)
                if C:
                    dve.wait_ge(S["x2_ready"], tc + 1)
                    stats(x2[:, :], c_st, c_mv, S["c_stat"], S["c_aggr"], tc)
                if G:
                    expert_weights(0)
                if A:
                    wait(dve, S["t_tr"], s)
                    normalise(a_xn[:, :], a_x[:, :], a_mv, a_r[:, 0:1], S["a_rstd"], S["a_xn_ready"], ta)
                if D:
                    dve.wait_ge(S["c_wo"], td + 1)
                    dve.wait_ge(S["c_kept"], td + 1)
                    dve.tensor_tensor(c_x3[:, :], M1[:, 2 * P:3 * P], c_x2[:, :], ALU.add).then_inc(S["x3_ready"], 1)
                if F:
                    dve.wait_ge(S["x1_ready"], tf + 1)
                    stats(x1[:, :], b_st, b_mv, S["b_stat"], S["b_aggr"], tf)
                if D:
                    dve.wait_ge(S["x3_ready"], td + 1)
                    stats(c_x3[:, :], d_st, d_mv, S["d_stat"], S["d_aggr"], td)
                if C:
                    wait(dve, S["t_tr"], s)
                    normalise(c_xn[:, :], x2[:, :], c_mv, c_r[:, 0:1], S["c_rstd"], S["c_xn_ready"], tc)
                if G:
                    expert_weights(1)
                if D:
                    normalise(d_y[:, :], c_x3[:, :], d_mv, d_r[:, 0:1], S["d_rstd"], S["d_y_ready"], td)
                if G:
                    expert_weights(2)
                if F:
                    wait(dve, S["b_tr"], tf)
                    normalise(b_xs[:, :], x1[:, :], b_mv, b_r[:, 5:6], S["b_p6"], S["b_xs_ready"], tf)
                if D:
                    dve.wait_ge(S["d_y_ready"], td + 1)
                    dve.tensor_reduce(d_s[:, 0:1], d_y[:, :], AX_X, ALU.max, apply_absolute_value=True)\
                        .then_inc(S["d_s1"], 1)
                if A:
                    dve.wait_ge(S["a_proj"], ta + 1)
                    dve.tensor_tensor(a_ropec[:, :], M1[:, 0:2 * P], cos_t, ALU.mult).then_inc(S["a_rs"], 1)
                if D:
                    dve.wait_ge(S["d_s1"], td + 1)
                    dve.tensor_scalar(d_s[:, 1:2], d_s[:, 0:1], 1e-12, 1.0 / QMAX, ALU.max, ALU.mult)\
                        .then_inc(S["d_s2"], 1)
                if A:
                    dve.wait_ge(S["a_proj"], ta + 1)
                    dve.tensor_tensor(a_ropes[:, :], M1[:, 2 * P:4 * P], sin_t, ALU.mult).then_inc(S["a_rs"], 1)
                if D:
                    dve.wait_ge(S["d_s2"], td + 1)
                    dve.reciprocal(d_s[:, 2:3], d_s[:, 1:2]).then_inc(S["d_s3"], 1)
                if A:
                    dve.wait_ge(S["a_rs"], 2 * ta + 2)
                    wait(dve, S["a_score"], GROUPS * ta)
                    dve.tensor_tensor(a_qkt[:, :], a_ropec[:, :], a_ropes[:, :], ALU.add).then_inc(S["a_qk_ready"], 1)
                if D:
                    dve.wait_ge(S["d_s3"], td + 1)
                    dve.tensor_scalar(d_yr[:, :], d_y[:, :], d_s[:, 2:3], ROUND, ALU.mult, ALU.add)\
                        .then_inc(S["d_yr_ready"], 1)
                if A:
                    dve.wait_ge(S["a_qk_ready"], ta + 1)
                    dve.tensor_tensor(a_kbd[:, :, :], a_qkt[:, P:2 * P].unsqueeze(1).to_broadcast([P, GROUP, P]),
                                      hmask.unsqueeze(2).to_broadcast([P, GROUP, P]), ALU.mult)\
                        .then_inc(S["a_kbd_ready"], 1)
                if G:
                    expert_weights(3)
                if A:
                    largest(0)
                if D:
                    dve.wait_ge(S["d_yr_ready"], td + 1)
                    dve.tensor_scalar(d_yc[:, :], d_yr[:, :], ROUND, QMAX, ALU.subtract, ALU.min)\
                        .then_inc(S["d_yc_ready"], 1)
                if A:
                    largest(1)
                if D:
                    dve.wait_ge(S["d_yc_ready"], td + 1)
                    dve.tensor_scalar(d_yq[:, :], d_yc[:, :], -QMAX, None, ALU.max).then_inc(S["d_yq_ready"], 1)
                if G:
                    expert_weights(4)
                if F:
                    wait(dve, S["b_cand_ready"], tf)
                    hold(dve, S["b_sim_ready"], tf + 1, S["dve_held"])
                    for i in range(2 * EH):
                        last = dve.max(b_top[:, i, 0:8], b_sim[:, i, :])
                    last.then_inc(S["b_t1"], 1)
                if A:
                    largest(2)
                if C:
                    dve.wait_ge(S["c_qt_ready"], tc + 1)
                    wait(dve, S["c_score"], GROUPS * tc)
                    for c in range(GROUP):
                        n = NK1[c]
                        last = dve.tensor_scalar(c_kbd[:, OFF1[c]:OFF1[c] + n], c_kt[:, 0:n], hmask[:, c:c + 1], None,
                                                 ALU.mult)
                    last.then_inc(S["c_kbd_ready"], 1)
                if A:
                    largest(3)
                if G:
                    expert_weights(5)
                if D:
                    dve.wait_ge(S["d_int"], td + 1)
                    dve.scalar_tensor_tensor(d_d[:, :], M0[:, P:2 * P], d_s[:, 1:2], rhs_row[:, :], ALU.mult, ALU.mult)\
                        .then_inc(S["d_d_ready"], 1)
                if F:
                    hold(dve, S["b_t1"], tf + 1, S["dve_held"])
                    for i in range(2 * EH):
                        last = dve.match_replace(b_rest[:, i, :], b_top[:, i, 0:8], b_sim[:, i, :], LOW)
                    last.then_inc(S["b_t2"], 1)
                if D:
                    dve.wait_ge(S["d_d_ready"], td + 1)
                    wait(dve, S["stored"], 16 * td)
                    dve.tensor_tensor(d_out[:, :], d_d[:, :], c_x3[:, :], ALU.add).then_inc(S["d_out_ready"], 1)
                if C:
                    dve.wait_ge(S["c_score"], GROUPS * tc + GROUPS)
                    sc = SC[:, :].rearrange("p (i k) -> p i k", k=512)[:, :, 0:2 * W1]\
                        .rearrange("p i (j k) -> p i j k", k=W1)
                    for c in range(GROUP):
                        last = dve.tensor_reduce(c_nmax[:, c, :].rearrange("p (j i) -> p i j", i=2),
                                                 sc[:, :, :, OFF1[c]:OFF1[c] + NK1[c]], AX_X, ALU.max, negate=True)
                    last.then_inc(S["c_max"], 1)
                if G:
                    expert_weights(6)
                if F:
                    hold(dve, S["b_t2"], tf + 1, S["dve_held"])
                    for i in range(2 * EH):
                        last = dve.max(b_top[:, i, 8:16], b_rest[:, i, :])
                    last.then_inc(S["b_t3"], 1)
                if G:
                    expert_weights(7)
                if A:
                    dve.wait_ge(S["a_pv"], GROUPS * ta + GROUPS)
                    heads = M1[:, 0:HEADS * VW].rearrange("p (h d) -> p h d", d=VW)
                    dve.reciprocal(a_rec[:, :], heads[:, :, DK]).then_inc(S["a_rec_ready"], 1)
                    dve.wait_ge(S["a_rec_ready"], ta + 1)
                    dve.tensor_tensor(a_o[:, :].rearrange("p (h d) -> p h d", d=DK), heads[:, :, 0:DK],
                                      a_rec[:, :].unsqueeze(2).to_broadcast([P, HEADS, DK]), ALU.mult)\
                        .then_inc(S["a_o_ready"], 1)
                if G:
                    weighted(0)
                if F:
                    hold(dve, S["b_cand_ready"], tf + 1, S["dve_held"])
                    for h in range(EH):
                        last = dve.max(b_ctop[:, h, 0:8], b_cand[:, h, :])
                    last.then_inc(S["b_c1"], 1)
                if A:
                    dve.wait_ge(S["a_wo"], ta + 1)
                    dve.wait_ge(S["a_xresin"], 16 * ta + 16)
                    if F:
                        dve.wait_ge(S["f_kept"], tf + 1)
                    dve.tensor_tensor(x1[:, :], M1[:, 2 * P:3 * P], a_xres[:, :], ALU.add).then_inc(S["x1_ready"], 1)
                if F:
                    hold(dve, S["b_c1"], tf + 1, S["dve_held"])
                    for h in range(EH):
                        last = dve.match_replace(b_crest[:, h, :], b_ctop[:, h, 0:8], b_cand[:, h, :], LOW)
                    last.then_inc(S["b_c2"], 1)
                if G:
                    weighted(1)
                if F:
                    hold(dve, S["b_c2"], tf + 1, S["dve_held"])
                    for h in range(EH):
                        last = dve.max(b_ctop[:, h, 8:16], b_crest[:, h, :])
                    last.then_inc(S["b_c3"], 1)
                if C:
                    dve.wait_ge(S["c_pv"], 2 * tc + 2)
                    heads = M1[:, 0:HEADS * VW].rearrange("p (h d) -> p h d", d=VW)
                    dve.reciprocal(c_rec[:, :], heads[:, :, DK]).then_inc(S["c_rec_ready"], 1)
                    dve.wait_ge(S["c_rec_ready"], tc + 1)
                    dve.tensor_tensor(c_o[:, :].rearrange("p (h d) -> p h d", d=DK), heads[:, :, 0:DK],
                                      c_rec[:, :].unsqueeze(2).to_broadcast([P, HEADS, DK]), ALU.mult)\
                        .then_inc(S["c_o_ready"], 1)
                if F:
                    dve.wait_ge(S["b_c3"], tf + 1)
                    dve.tensor_scalar(b_thr[:, :], b_ctop[:, :, TOP - 1], 0.0, None, ALU.max)\
                        .then_inc(S["b_thr_ready"], 1)
                if G:
                    dve.wait_ge(S["b_ffn"], 2 * tg + 2)
                    dve.wait_ge(S["g_kept"], tg + 1)
                    if C:
                        dve.wait_ge(S["c_kept"], tc + 1)
                    dve.tensor_tensor(x2[:, :], B0[:, 0:P], g_x1[:, :], ALU.add).then_inc(S["x2_ready"], 1)
            steps(dve, step)


ROUNDS = -(-SLOTS // 4)
LOADED = 19 * 16


_INS = ['x', 'ctx_1024', 'L0_xattn_W_q', 'L0_xattn_W_k', 'L0_xattn_W_v', 'L0_xattn_W_o', 'L0_ffn_norm_w', 'L0_ffn_wq',
        'L0_ffn_keys', 'L0_ffn_expert_down', 'L0_ffn_expert_up', 'L1_xattn_Wq', 'L1_xattn_bq', 'L1_xattn_Wk',
        'L1_xattn_bk', 'L1_xattn_Wv', 'L1_xattn_bv', 'L1_xattn_Wo', 'L1_xattn_bo', 'L1_ffn_rhs']


def constants():
    import numpy as np
    f = np.float32
    order = np.concatenate([np.arange(a, P, s) for a, s in ((0, 8), (4, 8), (2, 4), (1, 2))])
    inv_freq = f(1.0) / np.power(f(10000.0), np.arange(0, DK, 2, dtype=f) / f(DK)).astype(f)
    angle = np.outer(np.arange(P, dtype=f), inv_freq).astype(f)
    pair = (np.arange(P) % DK) // 2
    cos, sin = np.cos(angle).astype(f)[:, pair].T, np.sin(angle).astype(f)[:, pair].T
    sin = sin * np.where(np.arange(P) % 2 == 0, f(-1), f(1))[:, None]
    t = np.zeros((P, C_ALL), f)
    t[:, C_ID:C_ID + P] = np.eye(P, dtype=f)
    t[:, C_COS:C_COS + P], t[:, C_COS + P:C_COS + 2 * P] = cos * f(SCALE), cos[:, order]
    t[:, C_SIN:C_SIN + P], t[:, C_SIN + P:C_SIN + 2 * P] = sin * f(SCALE), sin[:, order]
    t[np.arange(P), C_MASK + np.arange(P) // DK % GROUP] = 1.0
    return t


def kernel(**inputs):
    import numpy as _np
    import concourse.bacc as _bacc
    from concourse import mybir as _mybir
    from concourse.bass_utils import run_bass_kernel_spmd as _run

    nc = _bacc.Bacc("TRN2", target_bir_lowering=False, num_devices=1)
    arrays = {f"in_{n}_dram": _np.ascontiguousarray(inputs[n]) for n in _INS}
    arrays["constants_dram"] = constants()
    args = [nc.dram_tensor(n, a.shape, _mybir.dt.from_np(a.dtype), kind="ExternalInput").ap() for n, a in arrays.items()]
    shape = arrays["in_x_dram"].shape
    out = nc.dram_tensor("out_dram", shape, _mybir.dt.float32, kind="ExternalOutput").ap()
    build(nc, *args, out)
    r = _run(nc, [arrays], core_ids=[0])
    return r.results[0]["out_dram"]
```

```python
from contextlib import ExitStack

import concourse.bass as bass
from concourse import mybir

F32 = mybir.dt.float32
BF16 = mybir.dt.bfloat16
ALU = mybir.AluOpType
ACT = mybir.ActivationFunctionType
AX_X = mybir.AxisListType.X

P = 128
HEADS = 16
DK = P // HEADS
VW = DK + 1
GROUP = 4
GROUPS = HEADS // GROUP
STRIDES = (1, 2, 4, 8)
NK1 = [P // s for s in STRIDES]
OFF1 = [sum(NK1[:c]) for c in range(GROUP)]
W1 = sum(NK1)
EH = 8
NKEY = 32
TOP = 16
EXPERTS = NKEY * NKEY
EC = EXPERTS // P
PAIRS = [(0, 1, 16), (1, 1, 8), (2, 1, 5), (3, 1, 4), (4, 1, 3), (5, 3, 2), (8, 8, 1)]
NCAND = sum(a * b for _, a, b in PAIRS)
EPS = 1e-5
QMAX = 127.0
ROUND = 12582912.0
LOW = -3.0e38
SCALE = 1.0 / float(DK) ** 0.5

WQ0, WK0, WV0, WO0, WQ1, WK1, WV1, WO1 = range(8)
KEYS, SUBQ, DOWN, RHS = 8, 12, 28, 36
SLOTS = 37
ROUNDS = [(SUBQ, 4), (SUBQ + 4, 4), (SUBQ + 8, 4), (SUBQ + 12, 4), (KEYS, 4), (DOWN, 4), (DOWN + 4, 4),
          (WQ0, 4), (WQ1, 4), (RHS, 1)]
FIRST_LOADED = 3 * 16
REST_LOADED = 16 * 16
C_ID, C_COS, C_SIN, C_MASK = 0, P, 3 * P, 5 * P
C_ALL = 5 * P + GROUP


def wait(eng, sem, value):
    if isinstance(value, int) and value <= 0:
        return
    eng.wait_ge(sem, value)


def hold(eng, sem, value, held):
    wait(eng, sem, value)
    eng.sem_inc(held, 1)


def build(nc, x, ctxt, wq0, wk0, wv0, wo0, norm_w, subq, keys, down, up,
          wq1, bq1, wk1, bk1, wv1, bv1, wo1, bo1, rhs, table, out):
    TILES = x.shape[0]

    with ExitStack() as stack:
        def sb(name, shape, dt=F32):
            return stack.enter_context(nc.sbuf_tensor(name, shape, dt))

        def bank(name, cols=512):
            return stack.enter_context(nc.psum_tensor(name, [P, cols], F32))

        def sem(name):
            return stack.enter_context(nc.semaphore(name))

        const = sb("const", [P, C_ALL])
        ident = const[:, C_ID:C_ID + P]
        rope_t = const[:, C_COS:C_COS + 4 * P]
        hmask = const[:, C_MASK:C_MASK + GROUP]
        raw = sb("raw", [P, SLOTS, P])
        wt = sb("wt", [P, SLOTS, P])
        swapped = sb("swapped", [P, 2, P])
        w_sim = sb("w_sim", [P, 2 * EH * NKEY])
        down_t = sb("down_t", [P, EC, P])
        up_sb = sb("up_sb", [P, EC, P])
        cols = sb("cols", [P, 8])
        bk_mask = sb("bk_mask", [P, GROUP])
        bv_rep = sb("bv_rep", [P, P])
        bo_rep = sb("bo_rep", [P, P])
        attn_bias = sb("attn_bias", [P, P])
        rhs_amax = sb("rhs_amax", [P, 4])
        rhs_r = sb("rhs_r", [P, P])
        rhs_srep = sb("rhs_srep", [P, P])
        rhs_q = sb("rhs_q", [P, P], BF16)
        rhs_row = sb("rhs_row", [P, P])
        neghalf = sb("neghalf", [P, 1])
        unused = sb("unused", [P, 1])

        a_x = sb("a_x", [P, P])
        a_xres = sb("a_xres", [P, P])
        a_ctx = sb("a_ctx", [P, P])
        a_st = sb("a_st", [P, 6])
        a_mv = sb("a_mv", [P, 2])
        a_r = sb("a_r", [P, 3])
        a_xn = sb("a_xn", [P, P])
        xct = sb("xct", [P, 4 * P])
        a_v = sb("a_v", [P, HEADS, VW])
        a_rope = sb("a_rope", [P, 4 * P])
        a_qkt = sb("a_qkt", [P, 2 * P])
        a_kbd = sb("a_kbd", [P, GROUP, P])
        a_nmax = sb("a_nmax", [P, HEADS])
        a_p = sb("a_p", [P, 2, GROUP * P])
        a_pt = sb("a_pt", [P, 2, GROUP * P])
        a_rec = sb("a_rec", [P, HEADS])
        a_o = sb("a_o", [P, P])
        a_ot = sb("a_ot", [P, P])
        x1 = sb("x1", [P, P])
        f_x1 = sb("f_x1", [P, P])
        g_x1 = sb("g_x1", [P, P])
        b_st = sb("b_st", [P, 6])
        b_mv = sb("b_mv", [P, 2])
        b_r = sb("b_r", [P, 8])
        b_xs = sb("b_xs", [P, P])
        b_xst = sb("b_xst", [P, P])
        b_g = sb("b_g", [P, EXPERTS])
        b_sim = sb("b_sim", [P, 2 * EH, NKEY])
        b_simg = sb("b_simg", [P, 2 * EH, NKEY])
        b_rest = sb("b_rest", [P, 2 * EH, NKEY])
        b_top = sb("b_top", [P, 2 * EH, TOP])
        b_cand = sb("b_cand", [P, EH, NCAND])
        b_crest = sb("b_crest", [P, EH, NCAND])
        b_ctop = sb("b_ctop", [P, EH, TOP])
        b_thr = sb("b_thr", [P, EH])
        NS = 4
        NW = 4
        b_sum = sb("b_sum", [P, NS, EXPERTS])
        b_w = sb("b_w", [P, NW, EXPERTS])
        b_cg = sb("b_cg", [P, EXPERTS])
        x2 = sb("x2", [P, P])
        c_x2 = sb("c_x2", [P, P])
        c_ctx = sb("c_ctx", [P, P])
        c_st = sb("c_st", [P, 6])
        c_mv = sb("c_mv", [P, 2])
        c_r = sb("c_r", [P, 3])
        c_xn = sb("c_xn", [P, P])
        c_ctxc = sb("c_ctxc", [P, P])
        c_qt = sb("c_qt", [P, P])
        c_va = sb("c_va", [P, GROUPS, VW])
        c_vb = sb("c_vb", [P, GROUPS, 3, VW])
        c_kbd = sb("c_kbd", [P, W1])
        c_nmax = sb("c_nmax", [P, GROUP, GROUPS])
        c_p = sb("c_p", [P, GROUPS, 2 * P])
        c_pt = sb("c_pt", [P, 2, 4 * P])
        c_rec = sb("c_rec", [P, HEADS])
        c_o = sb("c_o", [P, P])
        c_ot = sb("c_ot", [P, P])
        c_x3 = sb("c_x3", [P, P])
        d_st = sb("d_st", [P, 6])
        d_mv = sb("d_mv", [P, 2])
        d_r = sb("d_r", [P, 3])
        d_y = sb("d_y", [P, P])
        d_s = sb("d_s", [P, 3])
        d_yr = sb("d_yr", [P, P])
        d_yc = sb("d_yc", [P, P])
        d_yq = sb("d_yq", [P, P])
        d_yqt = sb("d_yqt", [P, P], BF16)
        d_d = sb("d_d", [P, P])
        d_out = sb("d_out", [P, P])

        M0 = bank("M0")
        M1 = bank("M1")
        SC = bank("SC", 1024)
        PT = bank("PT")
        H = bank("H", 1024)
        B0 = bank("B0")

        names = """first_loaded rest_loaded tr_done tr_copied w_ready sim_done bo_done rq_ready rq_done setup_dve setup_pool
        t_tr xct_ready
        a_xin a_xresin a_ctxin a_stat a_aggr a_eps a_rstd a_shift a_xn_ready a_proj a_vproj a_vready a_rope_ready
        a_qk_ready a_kbd_ready a_score a_max a_exp a_ptr a_ptcopy a_pv a_rec_ready a_o_ready a_otr a_ot_ready a_wo x1_ready
        f_kept g_kept b_stat b_aggr b_p1 b_p2 b_p3 b_p4 b_p5 b_p6 b_shift b_xs_ready b_tr b_xst_ready b_simmm b_sim_ready
        b_simg_ready b_t1 b_t2 b_t3 b_cand_ready b_c1 b_c2 b_c3 b_thr_ready
        b_hid b_gelu b_sum_ready b_w_ready b_wtr b_cg_ready b_ffn x2_ready
        c_ctxin c_kept c_stat c_aggr c_eps c_rstd c_shift c_xn_ready c_ctxc_ready c_qkproj c_vproj c_qt_ready
        c_v_ready c_kbd_ready c_score c_max c_exp c_ptr c_ptcopy c_pv c_rec_ready c_o_ready c_otr c_ot_ready c_wo x3_ready
        d_stat d_aggr d_eps d_rstd d_shift d_y_ready d_s1 d_s2 d_s3 d_yr_ready d_yc_ready d_yq_ready d_ytr
        d_yqt_ready d_int d_d_ready d_out_ready stored dve_held pool_held""".split()
        S = {n: sem(n) for n in names}

        block = stack.enter_context(nc.Block())

        def steps(eng, step):
            for s in range(5):
                step(s, True, s >= 1, s >= 2, s >= 3, s >= 4)
            with eng.Fori(5, TILES) as s:
                step(s, True, True, True, True, True)
            for s in range(TILES, TILES + 4):
                step(s, False, s < TILES + 1, s < TILES + 2, s < TILES + 3, True)

        @block.sync
        def _(sp):
            first = [
                (const[:, :], table),
                (raw[:, SUBQ:SUBQ + 16, :], subq.rearrange("i (c d) -> i c d", d=P)),
                (raw[:, KEYS:KEYS + 4, :], keys.rearrange("h k p d -> (h k p) d").rearrange("(c r) d -> r c d", r=P)),
            ]
            rest = [(raw[:, DOWN:DOWN + EC, :], down.rearrange("(c r) d -> r c d", r=P))]
            rest += [(raw[:, WQ0 + i, :], w) for i, w in enumerate((wq0, wk0, wv0, wo0, wq1, wk1, wv1, wo1))]
            rest += [
                (raw[:, RHS, :], rhs),
                (cols[:, 0:1], norm_w.rearrange("(p a) -> p a", a=1)),
                (cols[:, 1:2], bq1.rearrange("(p a) -> p a", a=1)),
                (cols[:, 2:3], bk1.rearrange("(p a) -> p a", a=1)),
                (cols[:, 3:4], bv1.rearrange("(p a) -> p a", a=1)),
                (bo_rep[:, :], bo1.rearrange("(a n) -> a n", a=1).to_broadcast([P, P])),
                (up_sb[:, :, :], up.rearrange("(c r) d -> r c d", r=P)),
            ]
            for to, of in first:
                sp.dma_start(to, of).then_inc(S["first_loaded"], 16)
            for to, of in rest:
                sp.dma_start(to, of).then_inc(S["rest_loaded"], 16)
            assert len(first) * 16 == FIRST_LOADED and len(rest) * 16 == REST_LOADED

            def load_ctx(to, t, arrived):
                for at, first, stride in ((0, 0, 8), (16, 4, 8), (32, 2, 4), (64, 1, 2)):
                    n = P // stride
                    sp.dma_start(to[at:at + n, :],
                                 ctxt[t, :, :].rearrange("(n s) d -> s n d", s=stride)[first]).then_inc(arrived, 16)

            def step(s, A, F, G, C, D):
                ta, tc, td = s, s - 3, s - 4
                if A:
                    wait(sp, S["a_xn_ready"], ta)
                    sp.dma_start(a_x[:, :], x[ta, :, :]).then_inc(S["a_xin"], 16)
                    wait(sp, S["t_tr"], s)
                    load_ctx(a_ctx, ta, S["a_ctxin"])
                if C:
                    wait(sp, S["t_tr"], s)
                    load_ctx(c_ctx, tc, S["c_ctxin"])
                if A:
                    wait(sp, S["x1_ready"], ta)
                    sp.dma_start(a_xres[:, :], x[ta, :, :]).then_inc(S["a_xresin"], 16)
                if D:
                    sp.wait_ge(S["d_out_ready"], td + 1)
                    sp.dma_start(out[td, :, :], d_out[:, :]).then_inc(S["stored"], 16)
            steps(sp, step)
            sp.wait_ge(S["stored"], 16 * TILES)

        @block.tensor
        def _(pe):
            pe.wait_ge(S["first_loaded"], FIRST_LOADED)
            banks = [M0[:, :], M1[:, :], PT[:, :], B0[:, :]]
            for r, (slot, n) in enumerate(ROUNDS):
                wait(pe, S["tr_copied"], r - 3)
                if slot == DOWN:
                    pe.wait_ge(S["rest_loaded"], REST_LOADED)
                for j in range(n):
                    last = pe.transpose(banks[r % 4][:, j * P:(j + 1) * P], raw[:, slot + j, :], ident)
                last.then_inc(S["tr_done"], 1)
            pe.wait_ge(S["tr_copied"], len(ROUNDS))
            for hp in range(2 * EH):
                h, half = hp // 2, hp % 2
                k0 = (h % 2) * 2 * NKEY + half
                last = pe.matmul(SC[:, hp * NKEY:(hp + 1) * NKEY], wt[:, SUBQ + hp, :],
                                 wt[:, KEYS + h // 2, k0:k0 + 2 * NKEY - 1:2], start=True, stop=True)
            last.then_inc(S["sim_done"], 1)
            pe.wait_ge(S["w_ready"], 1)
            pe.matmul(SC[:, 512:512 + P], bv_rep[:, :], wt[:, WO1, :], start=True, stop=True).then_inc(S["bo_done"], 1)
            pe.wait_ge(S["rq_ready"], 1)
            pe.transpose(H[:, 0:P], rhs_r[:, :], ident)
            pe.transpose(H[:, P:2 * P], rhs_srep[:, :], ident).then_inc(S["rq_done"], 1)
            pe.wait_ge(S["setup_dve"], 1)
            pe.wait_ge(S["setup_pool"], 4)

            def step(s, A, F, G, C, D):
                ta, tf, tg, tc, td = s, s - 1, s - 2, s - 3, s - 4

                def expert_head(h, half):
                    if h == 0:
                        pe.wait_ge(S["b_gelu"], 2 * tg + half + 1)
                    pe.wait_ge(S["b_w_ready"], EH * tg + h + 1)
                    for c in range(EC // 2 * half, EC // 2 * (half + 1)):
                        last = pe.matmul(H[:, c * P:(c + 1) * P], b_w[:, h % NW, c * P:(c + 1) * P], ident,
                                         start=(h == 0 and c % 4 == 0), stop=(h == EH - 1), is_transpose=True,
                                         skip_group_check=True)
                    last.then_inc(S["b_wtr"], 1)

                def hid(half):
                    wait(pe, S["b_cg_ready"], 2 * tg - 1 + half)
                    for c in range(EC // 2 * half, EC // 2 * (half + 1)):
                        last = pe.matmul(H[:, c * P:(c + 1) * P], down_t[:, c, :], b_xst[:, :], start=True, stop=True)
                    last.then_inc(S["b_hid"], 1)

                def score(g):
                    if g == 0:
                        pe.wait_ge(S["a_kbd_ready"], ta + 1)
                        wait(pe, S["c_exp"], 2 * tc)
                    if g >= 2:
                        pe.wait_ge(S["a_exp"], GROUPS * ta + g - 1)
                    pe.matmul(SC[:, (g % 2) * 512:(g % 2) * 512 + 512], a_qkt[32 * g:32 * g + 32, 0:P],
                              a_kbd[32 * g:32 * g + 32, :, :], start=True, stop=True).then_inc(S["a_score"], 1)

                def weights(g):
                    pe.wait_ge(S["a_exp"], GROUPS * ta + g + 1)
                    if g:
                        pe.wait_ge(S["a_ptcopy"], GROUPS * ta + g)
                    elif D:
                        pe.wait_ge(S["c_ptcopy"], 2 * td + 2)
                    for j in range(GROUP):
                        last = pe.transpose(PT[:, j * P:(j + 1) * P], a_p[:, g % 2, j * P:(j + 1) * P], ident)
                    last.then_inc(S["a_ptr"], 1)

                def weigh(g):
                    pe.wait_ge(S["a_ptcopy"], GROUPS * ta + g + 1)
                    if g == 0:
                        pe.wait_ge(S["a_vready"], ta + 1)
                    for j in range(GROUP):
                        h = GROUP * g + j
                        last = pe.matmul(M1[:, h * VW:(h + 1) * VW], a_pt[:, g % 2, j * P:(j + 1) * P], a_v[:, h, :],
                                         start=True, stop=True)
                    last.then_inc(S["a_pv"], 1)

                def ffn(half):
                    pe.wait_ge(S["b_cg_ready"], 2 * tg + half + 1)
                    if half == 0:
                        if C:
                            pe.wait_ge(S["c_qt_ready"], tc + 1)
                            pe.wait_ge(S["c_kbd_ready"], tc + 1)
                        if F:
                            pe.wait_ge(S["b_sim_ready"], tf + 1)
                    for c in range(EC // 2 * half, EC // 2 * (half + 1)):
                        last = pe.matmul(B0[:, 0:P], b_cg[:, c * P:(c + 1) * P], up_sb[:, c, :],
                                         start=(c == 0), stop=(c == EC - 1))
                    last.then_inc(S["b_ffn"], 1)

                def score1(g):
                    if g == 0:
                        pe.wait_ge(S["c_kbd_ready"], tc + 1)
                        pe.wait_ge(S["c_qt_ready"], tc + 1)
                    if g >= 2:
                        pe.wait_ge(S["c_score"], GROUPS * tc + g - 1)
                    elif A:
                        pe.wait_ge(S["a_exp"], GROUPS * ta + 3 + g)
                    sc = 512 * (g % 2) + W1 * (g // 2)
                    pe.matmul(SC[:, sc:sc + W1], c_qt[32 * g:32 * g + 32, :], c_kbd[32 * g:32 * g + 32, :],
                              start=True, stop=True).then_inc(S["c_score"], 1)

                def weights1(j):
                    pe.wait_ge(S["c_exp"], 2 * td + j + 1)
                    if j:
                        pe.wait_ge(S["c_ptcopy"], 2 * td + j)
                    else:
                        pe.wait_ge(S["a_ptcopy"], GROUPS * ta if A else GROUPS * TILES)
                    for i in range(4):
                        last = pe.transpose(PT[:, i * P:(i + 1) * P],
                                            c_p[:, 2 * j + i // 2, (i % 2) * P:(i % 2 + 1) * P], ident)
                    last.then_inc(S["c_ptr"], 1)

                def weigh1(j):
                    pe.wait_ge(S["c_ptcopy"], 2 * td + j + 1)
                    if j == 0:
                        pe.wait_ge(S["a_o_ready"], ta if A else TILES)
                    for i in range(2):
                        g = 2 * j + i
                        o = g * GROUP * VW
                        pe.matmul(M1[:, o:o + VW], c_pt[:, j, 2 * i * P:(2 * i + 1) * P], c_va[:, g, :],
                                  start=True, stop=True)
                        last = pe.matmul(M1[:, o + VW:o + GROUP * VW], c_pt[:, j, (2 * i + 1) * P:(2 * i + 2) * P],
                                         c_vb[:, g, :, :], start=True, stop=True)
                    last.then_inc(S["c_pv"], 1)

                if D:
                    weights1(0)
                if G:
                    hid(0)
                    hid(1)
                if D:
                    weights1(1)
                    weigh1(0)
                if G:
                    expert_head(0, 0)
                if D:
                    weigh1(1)
                if A or C:
                    wait(pe, S["d_d_ready"], td)
                    wait(pe, S["x1_ready"], ta if A else TILES)
                    if A:
                        pe.wait_ge(S["a_xn_ready"], ta + 1)
                        pe.wait_ge(S["a_ctxin"], 64 * ta + 64)
                        pe.transpose(M0[:, 0:P], a_xn[:, :], ident)
                        last = pe.transpose(M0[:, P:2 * P], a_ctx[:, :], ident)
                    if C:
                        pe.wait_ge(S["c_xn_ready"], tc + 1)
                        pe.wait_ge(S["c_ctxin"], 64 * tc + 64)
                        pe.transpose(M0[:, 2 * P:3 * P], c_xn[:, :], ident)
                        last = pe.transpose(M0[:, 3 * P:4 * P], c_ctx[:, :], ident)
                    last.then_inc(S["t_tr"], 1)
                if G:
                    expert_head(0, 1)
                    expert_head(1, 0)
                    expert_head(1, 1)
                if D:
                    pe.wait_ge(S["c_o_ready"], td + 1)
                    if C:
                        pe.wait_ge(S["c_ctxc_ready"], tc + 1)
                    if A or C:
                        pe.wait_ge(S["xct_ready"], s + 1)
                    pe.transpose(M0[:, 0:P], c_o[:, :], ident).then_inc(S["c_otr"], 1)
                if A:
                    pe.wait_ge(S["xct_ready"], s + 1)
                    if D:
                        pe.wait_ge(S["c_o_ready"], td + 1)
                    for i, w in enumerate((wt[:, WQ0, :], wt[:, WK0, :], swapped[:, 0, :], swapped[:, 1, :])):
                        last = pe.matmul(M1[:, i * P:(i + 1) * P], w, xct[:, (i % 2) * P:(i % 2 + 1) * P],
                                         start=True, stop=True)
                    last.then_inc(S["a_proj"], 1)
                if F:
                    pe.wait_ge(S["b_xs_ready"], tf + 1)
                    wait(pe, S["x2_ready"], tg)
                    pe.transpose(B0[:, 0:P], b_xs[:, :], ident).then_inc(S["b_tr"], 1)
                if D:
                    pe.wait_ge(S["c_ot_ready"], td + 1)
                    pe.matmul(M0[:, P:2 * P], c_ot[:, :], wt[:, WO1, :], start=True, stop=True)\
                        .then_inc(S["c_wo"], 1)
                if G:
                    expert_head(2, 0)
                if F:
                    pe.wait_ge(S["b_xst_ready"], tf + 1)
                    pe.matmul(B0[:, :], b_xst[:, :], w_sim[:, :], start=True, stop=True).then_inc(S["b_simmm"], 1)
                if A:
                    if C:
                        pe.wait_ge(S["c_ctxc_ready"], tc + 1)
                    if D:
                        pe.wait_ge(S["x3_ready"], td + 1)
                    pe.matmul(M0[:, 0:P], xct[:, P:2 * P], wt[:, WV0, :], start=True, stop=True)\
                        .then_inc(S["a_vproj"], 1)
                if G:
                    expert_head(2, 1)
                    expert_head(3, 0)
                if C:
                    pe.wait_ge(S["xct_ready"], s + 1)
                    pe.wait_ge(S["c_ctxc_ready"], tc + 1)
                    if D:
                        pe.wait_ge(S["x3_ready"], td + 1)
                    pe.matmul(M0[:, P:2 * P], xct[:, 3 * P:4 * P], wt[:, WV1, :], start=True, stop=True)
                    pe.matmul(M0[:, 2 * P:3 * P], c_ctxc[:, :], wt[:, WV1, :], start=True, stop=True)\
                        .then_inc(S["c_vproj"], 1)
                if A:
                    score(0)
                    score(1)
                if C:
                    if F:
                        pe.wait_ge(S["b_sim_ready"], tf + 1)
                    elif G:
                        pe.wait_ge(S["x2_ready"], tg)
                    pe.matmul(B0[:, 0:P], wt[:, WQ1, :], xct[:, 2 * P:3 * P], start=True, stop=True)
                    pe.matmul(B0[:, P:2 * P], wt[:, WK1, :], xct[:, 3 * P:4 * P], start=True, stop=True)\
                        .then_inc(S["c_qkproj"], 1)
                if G:
                    expert_head(3, 1)
                    expert_head(4, 0)
                if A:
                    score(2)
                    weights(0)
                if G:
                    expert_head(4, 1)
                if D:
                    pe.wait_ge(S["d_yq_ready"], td + 1)
                    if A:
                        pe.wait_ge(S["a_vready"], ta + 1)
                    if C:
                        pe.wait_ge(S["c_v_ready"], tc + 1)
                    pe.transpose(M0[:, 0:P], d_yq[:, :], ident).then_inc(S["d_ytr"], 1)
                if A:
                    score(3)
                if D:
                    pe.wait_ge(S["d_yqt_ready"], td + 1)
                    pe.matmul(M0[:, P:2 * P], d_yqt[:, :], rhs_q[:, :], start=True, stop=True).then_inc(S["d_int"], 1)
                if A:
                    weights(1)
                if G:
                    expert_head(5, 0)
                    expert_head(5, 1)
                    expert_head(6, 0)
                if A:
                    weigh(0)
                if C:
                    score1(0)
                if G:
                    expert_head(6, 1)
                if A:
                    weights(2)
                if C:
                    score1(1)
                    score1(2)
                    score1(3)
                if A:
                    weigh(1)
                    weights(3)
                if G:
                    expert_head(7, 0)
                    expert_head(7, 1)
                if A:
                    weigh(2)
                    weigh(3)
                if G:
                    ffn(0)
                if A:
                    pe.wait_ge(S["a_o_ready"], ta + 1)
                    if D:
                        pe.wait_ge(S["d_d_ready"], td + 1)
                    pe.transpose(M0[:, 0:P], a_o[:, :], ident).then_inc(S["a_otr"], 1)
                if G:
                    ffn(1)
                if A:
                    pe.wait_ge(S["a_ot_ready"], ta + 1)
                    pe.matmul(M0[:, P:2 * P], a_ot[:, :], wt[:, WO0, :], start=True, stop=True)\
                        .then_inc(S["a_wo"], 1)
            steps(pe, step)

        @block.scalar
        def _(act):
            act.wait_ge(S["setup_pool"], 4)
            act.activation(unused[:, :], neghalf[:, :], ACT.Exp)
            act.wait_ge(S["setup_dve"], 1)

            def copy(to, of):
                return act.activation(to, of, ACT.Copy)

            def normalise(to, src, factor, shift, ready, done, t):
                act.wait_ge(ready, t + 1)
                act.activation(to, src, ACT.Identity, bias=shift, scale=factor).then_inc(done, 1)

            def step(s, A, F, G, C, D):
                ta, tf, tg, tc, td = s, s - 1, s - 2, s - 3, s - 4

                def load_table(function):
                    act.activation(unused[:, :], neghalf[:, :], function)

                def gelu(half):
                    act.wait_ge(S["b_hid"], 2 * tg + half + 1)
                    lo, hi = half * 512, half * 512 + 512
                    act.activation(b_g[:, lo:hi], H[:, lo:hi], ACT.Gelu).then_inc(S["b_gelu"], 1)

                def exps(g):
                    act.wait_ge(S["a_max"], GROUPS * ta + g + 1)
                    if g >= 2:
                        act.wait_ge(S["a_ptr"], GROUPS * ta + g - 1)
                    for j in range(GROUP):
                        h = GROUP * g + j
                        sc = (g % 2) * 512 + j * P
                        last = act.activation(a_p[:, g % 2, j * P:(j + 1) * P], SC[:, sc:sc + P], ACT.Exp,
                                              bias=a_nmax[:, h:h + 1])
                    last.then_inc(S["a_exp"], 1)

                def take(g):
                    act.wait_ge(S["a_ptr"], GROUPS * ta + g + 1)
                    copy(a_pt[:, g % 2, :], PT[:, :]).then_inc(S["a_ptcopy"], 1)

                def exps1(j):
                    if j == 0:
                        act.wait_ge(S["c_max"], tc + 1)
                    for i in range(2):
                        g = 2 * j + i
                        for c in range(GROUP):
                            sc = 512 * i + j * W1 + OFF1[c]
                            last = act.activation(c_p[:, g, OFF1[c]:OFF1[c] + NK1[c]], SC[:, sc:sc + NK1[c]],
                                                  ACT.Exp, bias=c_nmax[:, c, g:g + 1])
                    last.then_inc(S["c_exp"], 1)

                def take1(j):
                    act.wait_ge(S["c_ptr"], 2 * td + j + 1)
                    copy(c_pt[:, j, :], PT[:, :]).then_inc(S["c_ptcopy"], 1)

                if D:
                    take1(0)
                if G:
                    gelu(0)
                    gelu(1)
                if D:
                    take1(1)
                if C:
                    wait(act, S["t_tr"], s)
                    normalise(c_xn[:, :], x2[:, :], c_r[:, 0:1], c_r[:, 2:3], S["c_shift"], S["c_xn_ready"], tc)
                if A:
                    wait(act, S["t_tr"], s)
                    normalise(a_xn[:, :], a_x[:, :], a_r[:, 0:1], a_r[:, 2:3], S["a_shift"], S["a_xn_ready"], ta)
                if C:
                    act.wait_ge(S["t_tr"], s + 1)
                    for at, n in ((0, 64), (64, 32), (96, 32)):
                        last = copy(c_ctxc[:, at:at + n], M0[:, 3 * P:3 * P + n])
                    last.then_inc(S["c_ctxc_ready"], 1)
                if A or C:
                    act.wait_ge(S["t_tr"], s + 1)
                    if A:
                        wait(act, S["a_vproj"], ta)
                    if C:
                        wait(act, S["c_qkproj"], tc)
                    lo, hi = (0 if A else 2 * P), (4 * P if C else 2 * P)
                    copy(xct[:, lo:hi], M0[:, lo:hi]).then_inc(S["xct_ready"], 1)
                if F:
                    wait(act, S["b_tr"], tf)
                    normalise(b_xs[:, :], x1[:, :], b_r[:, 5:6], b_r[:, 6:7], S["b_shift"], S["b_xs_ready"], tf)
                if D:
                    act.wait_ge(S["c_otr"], td + 1)
                    copy(c_ot[:, :], M0[:, 0:P]).then_inc(S["c_ot_ready"], 1)
                if F:
                    act.wait_ge(S["b_tr"], tf + 1)
                    copy(b_xst[:, :], B0[:, 0:P]).then_inc(S["b_xst_ready"], 1)
                    act.wait_ge(S["b_simmm"], tf + 1)
                    wait(act, S["b_t2"], tf)
                    copy(b_sim[:, :, :], B0[:, :].rearrange("p (h k) -> p h k", k=NKEY)).then_inc(S["b_sim_ready"], 1)
                if G:
                    load_table(ACT.Exp)
                if D:
                    wait(act, S["d_yr_ready"], td)
                    normalise(d_y[:, :], c_x3[:, :], d_r[:, 0:1], d_r[:, 2:3], S["d_shift"], S["d_y_ready"], td)
                if A:
                    exps(0)
                    act.wait_ge(S["a_vproj"], ta + 1)
                    if C:
                        act.wait_ge(S["c_vproj"], tc + 1)
                    copy(a_v[:, :, 0:DK], M0[:, 0:P].rearrange("p (h d) -> p h d", d=DK)).then_inc(S["a_vready"], 1)
                if C:
                    act.wait_ge(S["c_qkproj"], tc + 1)
                    wait(act, S["c_score"], GROUPS * tc)
                    act.activation(c_qt[:, :], B0[:, 0:P], ACT.Identity, bias=cols[:, 4:5], scale=SCALE)\
                        .then_inc(S["c_qt_ready"], 1)
                if A:
                    exps(1)
                if C:
                    act.wait_ge(S["c_vproj"], tc + 1)
                    if A:
                        act.wait_ge(S["a_vproj"], ta + 1)
                    wait(act, S["c_pv"], 2 * tc)
                    va = M0[:, P:2 * P].rearrange("p (g c d) -> p g c d", c=GROUP, d=DK)
                    vb = M0[:, 2 * P:3 * P].rearrange("p (g c d) -> p g c d", c=GROUP, d=DK)
                    copy(c_va[:, :, 0:DK], va[:, :, 0, :])
                    for i, (p0, p1) in enumerate(((0, 64), (64, 96), (96, 128))):
                        last = copy(c_vb[p0:p1, :, i, 0:DK], vb[p0:p1, :, i + 1, :])
                    last.then_inc(S["c_v_ready"], 1)
                if A:
                    take(0)
                if G:
                    wait(act, S["x2_ready"], tg)
                    copy(g_x1[:, :], f_x1[:, :]).then_inc(S["g_kept"], 1)
                if D:
                    act.wait_ge(S["d_ytr"], td + 1)
                    copy(d_yqt[:, :], M0[:, 0:P]).then_inc(S["d_yqt_ready"], 1)
                if C:
                    act.wait_ge(S["c_qkproj"], tc + 1)
                    wait(act, S["c_score"], GROUPS * tc)
                    for c in range(GROUP):
                        last = act.activation(c_kbd[:, OFF1[c]:OFF1[c] + NK1[c]], B0[:, P:P + NK1[c]], ACT.Identity,
                                              bias=bk_mask[:, c:c + 1], scale=hmask[:, c:c + 1])
                    last.then_inc(S["c_kbd_ready"], 1)
                if F:
                    act.wait_ge(S["b_sim_ready"], tf + 1)
                    wait(act, S["b_sum_ready"], EH * tf)
                    copy(b_simg[:, :, :], b_sim[:, :, :]).then_inc(S["b_simg_ready"], 1)
                if A:
                    exps(2)
                    take(1)
                    exps(3)
                    take(2)
                if F:
                    act.wait_ge(S["x1_ready"], tf + 1)
                    if G:
                        act.wait_ge(S["g_kept"], tg + 1)
                    copy(f_x1[:, :], x1[:, :]).then_inc(S["f_kept"], 1)
                if A:
                    take(3)
                if C:
                    exps1(0)
                    exps1(1)
                if A:
                    act.wait_ge(S["a_otr"], ta + 1)
                    copy(a_ot[:, :], M0[:, 0:P]).then_inc(S["a_ot_ready"], 1)
                if C:
                    load_table(ACT.Gelu)
            steps(act, step)

        @block.gpsimd
        def _(pool):
            pool.memset(neghalf[:, :], -0.5)
            pool.memset(a_v[:, :, DK:VW], 1.0)
            pool.memset(c_va[:, :, DK:VW], 1.0)
            pool.memset(c_vb[:, :, :, :], 0.0)
            pool.memset(c_p[:, :, W1:2 * P], 0.0).then_inc(S["setup_pool"], 1)
            pool.wait_ge(S["setup_pool"], 1)
            for i, (p0, p1) in enumerate(((0, 64), (64, 96), (96, 128))):
                pool.memset(c_vb[p0:p1, :, i, DK:VW], 1.0).then_inc(S["setup_pool"], 1)
                pool.wait_ge(S["setup_pool"], i + 2)
            pool.wait_ge(S["setup_dve"], 1)

            def add_eps(mv, r, aggr, eps, t):
                hold(pool, aggr, t + 1, S["pool_held"])
                pool.tensor_scalar(r[:, 1:2], mv[:, 1:2], EPS, None, ALU.add).then_inc(eps, 1)

            def inverse_root(r, eps, rstd, t):
                pool.wait_ge(eps, t + 1)
                pool.tensor_tensor(r[:, 0:1], r[:, 1:2], neghalf[:, :], ALU.pow).then_inc(rstd, 1)

            def mean_shift(mv, factor, shift, ready, done, t):
                hold(pool, ready, t + 1, S["pool_held"])
                pool.tensor_scalar(shift, mv[:, 0:1], factor, -1.0, ALU.mult, ALU.mult).then_inc(done, 1)

            def pair_sums(t, h):
                if h == 0:
                    pool.wait_ge(S["b_simg_ready"], t + 1)
                wait(pool, S["b_w_ready"], EH * t + h + 1 - NS)
                pool.tensor_tensor(
                    b_sum[:, h % NS, :].rearrange("p (i j) -> p i j", j=NKEY),
                    b_simg[:, 2 * h, :].unsqueeze(2).to_broadcast([P, NKEY, NKEY]),
                    b_simg[:, 2 * h + 1, :].unsqueeze(1).to_broadcast([P, NKEY, NKEY]),
                    ALU.add).then_inc(S["b_sum_ready"], 1)

            def step(s, A, F, G, C, D):
                ta, tf, tg, tc, td = s, s - 1, s - 2, s - 3, s - 4
                if C:
                    add_eps(c_mv, c_r, S["c_aggr"], S["c_eps"], tc)
                    inverse_root(c_r, S["c_eps"], S["c_rstd"], tc)
                if A:
                    add_eps(a_mv, a_r, S["a_aggr"], S["a_eps"], ta)
                if C:
                    mean_shift(c_mv, c_r[:, 0:1], c_r[:, 2:3], S["c_rstd"], S["c_shift"], tc)
                if A:
                    inverse_root(a_r, S["a_eps"], S["a_rstd"], ta)
                if F:
                    hold(pool, S["b_aggr"], tf + 1, S["pool_held"])
                    pool.tensor_scalar(b_r[:, 0:1], b_mv[:, 1:2], EPS, None, ALU.add).then_inc(S["b_p1"], 1)
                if A:
                    mean_shift(a_mv, a_r[:, 0:1], a_r[:, 2:3], S["a_rstd"], S["a_shift"], ta)
                if F:
                    pool.wait_ge(S["b_p1"], tf + 1)
                    pool.tensor_tensor(b_r[:, 1:2], b_r[:, 0:1], neghalf[:, :], ALU.pow).then_inc(S["b_p2"], 1)
                    hold(pool, S["b_p2"], tf + 1, S["pool_held"])
                    pool.tensor_scalar(b_r[:, 2:3], b_mv[:, 1:2], b_r[:, 1:2], b_r[:, 1:2], ALU.mult, ALU.mult)\
                        .then_inc(S["b_p3"], 1)
                    hold(pool, S["b_p3"], tf + 1, S["pool_held"])
                    pool.tensor_scalar(b_r[:, 3:4], b_r[:, 2:3], EPS, None, ALU.add).then_inc(S["b_p4"], 1)
                    pool.wait_ge(S["b_p4"], tf + 1)
                    pool.tensor_tensor(b_r[:, 4:5], b_r[:, 3:4], neghalf[:, :], ALU.pow).then_inc(S["b_p5"], 1)
                    pool.wait_ge(S["b_p5"], tf + 1)
                    pool.tensor_tensor(b_r[:, 5:6], b_r[:, 1:2], b_r[:, 4:5], ALU.mult).then_inc(S["b_p6"], 1)
                    mean_shift(b_mv, b_r[:, 5:6], b_r[:, 6:7], S["b_p6"], S["b_shift"], tf)
                if G:
                    pair_sums(tg, 4)
                if A:
                    pool.wait_ge(S["a_rope_ready"], ta + 1)
                    wait(pool, S["a_score"], GROUPS * ta)
                    pool.tensor_tensor(a_qkt[:, :], a_rope[:, 0:2 * P], a_rope[:, 2 * P:4 * P], ALU.add)\
                        .then_inc(S["a_qk_ready"], 1)
                    pool.wait_ge(S["a_qk_ready"], ta + 1)
                    pool.tensor_tensor(a_kbd[:, :, :], a_qkt[:, P:2 * P].unsqueeze(1).to_broadcast([P, GROUP, P]),
                                       hmask.unsqueeze(2).to_broadcast([P, GROUP, P]), ALU.mult)\
                        .then_inc(S["a_kbd_ready"], 1)
                if D:
                    add_eps(d_mv, d_r, S["d_aggr"], S["d_eps"], td)
                    inverse_root(d_r, S["d_eps"], S["d_rstd"], td)
                    mean_shift(d_mv, d_r[:, 0:1], d_r[:, 2:3], S["d_rstd"], S["d_shift"], td)
                if G:
                    pair_sums(tg, 5)
                    pair_sums(tg, 6)
                    pair_sums(tg, 7)
                if D:
                    pool.wait_ge(S["d_d_ready"], td + 1)
                    wait(pool, S["stored"], 16 * td)
                    pool.tensor_tensor(d_out[:, :], d_d[:, :], c_x3[:, :], ALU.add).then_inc(S["d_out_ready"], 1)
                if F:
                    pair_sums(tf, 0)
                    pair_sums(tf, 1)
                    pool.wait_ge(S["b_t3"], tf + 1)
                    wait(pool, S["b_c2"], tf)
                    halves = b_top[:, :, :].rearrange("p (h a) k -> p h a k", a=2)
                    at = 0
                    for i, ni, nj in PAIRS:
                        to = b_cand[:, :, at:at + ni * nj]
                        if ni == 1:
                            one = halves[:, :, 0, i:i + 1].to_broadcast([P, EH, nj])
                            two = halves[:, :, 1, 0:nj]
                        elif nj == 1:
                            one = halves[:, :, 0, i:i + ni]
                            two = halves[:, :, 1, 0:1].to_broadcast([P, EH, ni])
                        else:
                            to = to.rearrange("p h (i j) -> p h i j", j=nj)
                            one = halves[:, :, 0, i:i + ni].unsqueeze(3).to_broadcast([P, EH, ni, nj])
                            two = halves[:, :, 1, 0:nj].unsqueeze(2).to_broadcast([P, EH, ni, nj])
                        last = pool.tensor_tensor(to, one, two, ALU.add)
                        at += ni * nj
                    last.then_inc(S["b_cand_ready"], 1)
                    pair_sums(tf, 2)
                if C:
                    wait(pool, S["x3_ready"], tc)
                    pool.tensor_tensor(c_x2[:, :], x2[:, :], attn_bias[:, :], ALU.add).then_inc(S["c_kept"], 1)
                if F:
                    pair_sums(tf, 3)
            steps(pool, step)

        @block.vector
        def _(dve):
            banks = [M0[:, :], M1[:, :], PT[:, :], B0[:, :]]
            for r, (slot, n) in enumerate(ROUNDS):
                dve.wait_ge(S["tr_done"], r + 1)
                dve.tensor_copy(wt[:, slot:slot + n, :].rearrange("p a b -> p (a b)"),
                                banks[r % 4][:, 0:n * P]).then_inc(S["tr_copied"], 1)
            dve.wait_ge(S["rest_loaded"], REST_LOADED)
            dve.tensor_scalar(cols[:, 4:5], cols[:, 1:2], SCALE, None, ALU.mult)
            dve.tensor_scalar(bk_mask[:, :], hmask, cols[:, 2:3], None, ALU.mult)
            dve.tensor_copy(bv_rep[:, :], cols[:, 3:4].to_broadcast([P, P])).then_inc(S["w_ready"], 1)
            dve.wait_ge(S["tr_copied"], len(ROUNDS))
            for i, w in enumerate((WQ0, WK0)):
                pair = wt[:, w, :].rearrange("p (n a) -> p n a", a=2)
                for a in range(2):
                    dve.tensor_copy(swapped[:, i, :].rearrange("p (n a) -> p n a", a=2)[:, :, a], pair[:, :, 1 - a])
            dve.tensor_scalar(down_t[:, :, :], wt[:, DOWN:DOWN + EC, :], cols[:, 0:1], None, ALU.mult)
            dve.tensor_reduce(rhs_amax[:, 0:1], wt[:, RHS, :], AX_X, ALU.max, apply_absolute_value=True)\
                .then_inc(S["w_ready"], 1)
            dve.wait_ge(S["w_ready"], 2)
            dve.tensor_scalar(rhs_amax[:, 1:2], rhs_amax[:, 0:1], 1e-12, 1.0 / QMAX, ALU.max, ALU.mult)\
                .then_inc(S["w_ready"], 1)
            dve.wait_ge(S["w_ready"], 3)
            dve.reciprocal(rhs_amax[:, 2:3], rhs_amax[:, 1:2]).then_inc(S["w_ready"], 1)
            dve.tensor_copy(rhs_srep[:, :], rhs_amax[:, 1:2].to_broadcast([P, P]))
            dve.wait_ge(S["w_ready"], 4)
            dve.tensor_scalar(rhs_r[:, :], wt[:, RHS, :], rhs_amax[:, 2:3], ROUND, ALU.mult, ALU.add)\
                .then_inc(S["w_ready"], 1)
            dve.wait_ge(S["w_ready"], 5)
            dve.tensor_scalar(rhs_r[:, :], rhs_r[:, :], ROUND, QMAX, ALU.subtract, ALU.min).then_inc(S["w_ready"], 1)
            dve.wait_ge(S["w_ready"], 6)
            dve.tensor_scalar(rhs_r[:, :], rhs_r[:, :], -QMAX, None, ALU.max).then_inc(S["rq_ready"], 1)
            dve.wait_ge(S["sim_done"], 1)
            dve.tensor_scalar(w_sim[:, :], SC[:, 0:512], cols[:, 0:1], None, ALU.mult)
            dve.wait_ge(S["bo_done"], 1)
            dve.tensor_tensor(attn_bias[:, :], SC[:, 512:512 + P], bo_rep[:, :], ALU.add)
            dve.wait_ge(S["rq_done"], 1)
            dve.tensor_copy(rhs_q[:, :], H[:, 0:P])
            dve.tensor_copy(rhs_row[:, :], H[:, P:2 * P]).then_inc(S["setup_dve"], 1)
            dve.wait_ge(S["setup_dve"], 1)

            def row_stats(src, st, stat):
                dve.bn_stats(st[:, :], src).then_inc(stat, 1)

            def mean_var(st, mv, stat, aggr, t):
                hold(dve, stat, t + 1, S["dve_held"])
                dve.bn_aggr(mv[:, :], st[:, :]).then_inc(aggr, 1)

            def step(s, A, F, G, C, D):
                ta, tf, tg, tc, td = s, s - 1, s - 2, s - 3, s - 4

                def expert_weights(h):
                    dve.wait_ge(S["b_sum_ready"], EH * tg + h + 1)
                    wait(dve, S["b_wtr"], 2 * (EH * tg + h + 1 - NW))
                    dve.scalar_tensor_tensor(b_w[:, h % NW, :], b_sum[:, h % NS, :], b_thr[:, h:h + 1],
                                             b_sum[:, h % NS, :], ALU.is_ge, ALU.mult).then_inc(S["b_w_ready"], 1)

                def weighted(half):
                    dve.wait_ge(S["b_wtr"], 2 * (EH * tg + EH) - 1 + half)
                    wait(dve, S["b_ffn"], 2 * tg - 1 + half)
                    lo, hi = half * 512, half * 512 + 512
                    dve.tensor_tensor(b_cg[:, lo:hi], H[:, lo:hi], b_g[:, lo:hi], ALU.mult).then_inc(S["b_cg_ready"], 1)

                def largest(g):
                    dve.wait_ge(S["a_score"], GROUPS * ta + g + 1)
                    dve.tensor_reduce(a_nmax[:, GROUP * g:GROUP * (g + 1)],
                                      SC[:, (g % 2) * 512:(g % 2) * 512 + 512].rearrange("p (h k) -> p h k", k=P),
                                      AX_X, ALU.max, negate=True).then_inc(S["a_max"], 1)

                if C:
                    dve.wait_ge(S["x2_ready"], tc + 1)
                    row_stats(x2[:, :], c_st, S["c_stat"])
                if A:
                    dve.wait_ge(S["a_xin"], 16 * ta + 16)
                    row_stats(a_x[:, :], a_st, S["a_stat"])
                if C:
                    mean_var(c_st, c_mv, S["c_stat"], S["c_aggr"], tc)
                if F:
                    dve.wait_ge(S["x1_ready"], tf + 1)
                    row_stats(x1[:, :], b_st, S["b_stat"])
                if A:
                    mean_var(a_st, a_mv, S["a_stat"], S["a_aggr"], ta)
                if G:
                    expert_weights(0)
                if F:
                    mean_var(b_st, b_mv, S["b_stat"], S["b_aggr"], tf)
                if G:
                    expert_weights(1)
                    expert_weights(2)
                if D:
                    dve.wait_ge(S["c_pv"], 2 * td + 2)
                    heads = M1[:, 0:HEADS * VW].rearrange("p (h d) -> p h d", d=VW)
                    dve.reciprocal(c_rec[:, :], heads[:, :, DK]).then_inc(S["c_rec_ready"], 1)
                    dve.wait_ge(S["c_rec_ready"], td + 1)
                    dve.tensor_tensor(c_o[:, :].rearrange("p (h d) -> p h d", d=DK), heads[:, :, 0:DK],
                                      c_rec[:, :].unsqueeze(2).to_broadcast([P, HEADS, DK]), ALU.mult)\
                        .then_inc(S["c_o_ready"], 1)
                if G:
                    expert_weights(3)
                if A:
                    dve.wait_ge(S["a_proj"], ta + 1)
                    wait(dve, S["a_qk_ready"], ta)
                    dve.tensor_tensor(a_rope[:, :], M1[:, :], rope_t, ALU.mult).then_inc(S["a_rope_ready"], 1)
                if D:
                    dve.wait_ge(S["c_wo"], td + 1)
                    dve.wait_ge(S["c_kept"], td + 1)
                    wait(dve, S["d_out_ready"], td)
                    dve.tensor_tensor(c_x3[:, :], M0[:, P:2 * P], c_x2[:, :], ALU.add).then_inc(S["x3_ready"], 1)
                    dve.wait_ge(S["x3_ready"], td + 1)
                    row_stats(c_x3[:, :], d_st, S["d_stat"])
                if G:
                    expert_weights(4)
                if D:
                    mean_var(d_st, d_mv, S["d_stat"], S["d_aggr"], td)
                if F:
                    wait(dve, S["b_cand_ready"], tf)
                    hold(dve, S["b_sim_ready"], tf + 1, S["dve_held"])
                    for i in range(2 * EH):
                        last = dve.max(b_top[:, i, 0:8], b_sim[:, i, :])
                    last.then_inc(S["b_t1"], 1)
                if A:
                    largest(0)
                if D:
                    dve.wait_ge(S["d_y_ready"], td + 1)
                    dve.tensor_reduce(d_s[:, 0:1], d_y[:, :], AX_X, ALU.max, apply_absolute_value=True)\
                        .then_inc(S["d_s1"], 1)
                    dve.wait_ge(S["d_s1"], td + 1)
                    dve.tensor_scalar(d_s[:, 1:2], d_s[:, 0:1], 1e-12, 1.0 / QMAX, ALU.max, ALU.mult)\
                        .then_inc(S["d_s2"], 1)
                if A:
                    largest(1)
                if D:
                    dve.wait_ge(S["d_s2"], td + 1)
                    dve.reciprocal(d_s[:, 2:3], d_s[:, 1:2]).then_inc(S["d_s3"], 1)
                    dve.wait_ge(S["d_s3"], td + 1)
                    dve.tensor_scalar(d_yr[:, :], d_y[:, :], d_s[:, 2:3], ROUND, ALU.mult, ALU.add)\
                        .then_inc(S["d_yr_ready"], 1)
                if G:
                    expert_weights(5)
                if D:
                    dve.wait_ge(S["d_yr_ready"], td + 1)
                    dve.tensor_scalar(d_yc[:, :], d_yr[:, :], ROUND, QMAX, ALU.subtract, ALU.min)\
                        .then_inc(S["d_yc_ready"], 1)
                    dve.wait_ge(S["d_yc_ready"], td + 1)
                    dve.tensor_scalar(d_yq[:, :], d_yc[:, :], -QMAX, None, ALU.max).then_inc(S["d_yq_ready"], 1)
                if A:
                    largest(2)
                if G:
                    expert_weights(6)
                if D:
                    dve.wait_ge(S["d_int"], td + 1)
                    dve.scalar_tensor_tensor(d_d[:, :], M0[:, P:2 * P], d_s[:, 1:2], rhs_row[:, :], ALU.mult, ALU.mult)\
                        .then_inc(S["d_d_ready"], 1)
                if A:
                    largest(3)
                if F:
                    hold(dve, S["b_t1"], tf + 1, S["dve_held"])
                    for i in range(2 * EH):
                        last = dve.match_replace(b_rest[:, i, :], b_top[:, i, 0:8], b_sim[:, i, :], LOW)
                    last.then_inc(S["b_t2"], 1)
                if G:
                    expert_weights(7)
                if F:
                    hold(dve, S["b_t2"], tf + 1, S["dve_held"])
                    for i in range(2 * EH):
                        last = dve.max(b_top[:, i, 8:16], b_rest[:, i, :])
                    last.then_inc(S["b_t3"], 1)
                if C:
                    dve.wait_ge(S["c_score"], GROUPS * tc + GROUPS)
                    sc = SC[:, :].rearrange("p (i k) -> p i k", k=512)[:, :, 0:2 * W1]\
                        .rearrange("p i (j k) -> p i j k", k=W1)
                    for c in range(GROUP):
                        last = dve.tensor_reduce(c_nmax[:, c, :].rearrange("p (j i) -> p i j", i=2),
                                                 sc[:, :, :, OFF1[c]:OFF1[c] + NK1[c]], AX_X, ALU.max, negate=True)
                    last.then_inc(S["c_max"], 1)
                if G:
                    weighted(0)
                    weighted(1)
                if F:
                    hold(dve, S["b_cand_ready"], tf + 1, S["dve_held"])
                    for h in range(EH):
                        last = dve.max(b_ctop[:, h, 0:8], b_cand[:, h, :])
                    last.then_inc(S["b_c1"], 1)
                if A:
                    dve.wait_ge(S["a_pv"], GROUPS * ta + GROUPS)
                    heads = M1[:, 0:HEADS * VW].rearrange("p (h d) -> p h d", d=VW)
                    dve.reciprocal(a_rec[:, :], heads[:, :, DK]).then_inc(S["a_rec_ready"], 1)
                    dve.wait_ge(S["a_rec_ready"], ta + 1)
                    dve.tensor_tensor(a_o[:, :].rearrange("p (h d) -> p h d", d=DK), heads[:, :, 0:DK],
                                      a_rec[:, :].unsqueeze(2).to_broadcast([P, HEADS, DK]), ALU.mult)\
                        .then_inc(S["a_o_ready"], 1)
                if F:
                    hold(dve, S["b_c1"], tf + 1, S["dve_held"])
                    for h in range(EH):
                        last = dve.match_replace(b_crest[:, h, :], b_ctop[:, h, 0:8], b_cand[:, h, :], LOW)
                    last.then_inc(S["b_c2"], 1)
                    hold(dve, S["b_c2"], tf + 1, S["dve_held"])
                    for h in range(EH):
                        last = dve.max(b_ctop[:, h, 8:16], b_crest[:, h, :])
                    last.then_inc(S["b_c3"], 1)
                if G:
                    dve.wait_ge(S["b_ffn"], 2 * tg + 2)
                    dve.wait_ge(S["g_kept"], tg + 1)
                    if C:
                        dve.wait_ge(S["c_kept"], tc + 1)
                    dve.tensor_tensor(x2[:, :], B0[:, 0:P], g_x1[:, :], ALU.add).then_inc(S["x2_ready"], 1)
                if F:
                    dve.wait_ge(S["b_c3"], tf + 1)
                    dve.tensor_scalar(b_thr[:, :], b_ctop[:, :, TOP - 1], 0.0, None, ALU.max)\
                        .then_inc(S["b_thr_ready"], 1)
                if A:
                    dve.wait_ge(S["a_wo"], ta + 1)
                    dve.wait_ge(S["a_xresin"], 16 * ta + 16)
                    if F:
                        dve.wait_ge(S["f_kept"], tf + 1)
                    dve.tensor_tensor(x1[:, :], M0[:, P:2 * P], a_xres[:, :], ALU.add).then_inc(S["x1_ready"], 1)
            steps(dve, step)



_INS = ['x', 'ctx_1024', 'L0_xattn_W_q', 'L0_xattn_W_k', 'L0_xattn_W_v', 'L0_xattn_W_o', 'L0_ffn_norm_w', 'L0_ffn_wq',
        'L0_ffn_keys', 'L0_ffn_expert_down', 'L0_ffn_expert_up', 'L1_xattn_Wq', 'L1_xattn_bq', 'L1_xattn_Wk',
        'L1_xattn_bk', 'L1_xattn_Wv', 'L1_xattn_bv', 'L1_xattn_Wo', 'L1_xattn_bo', 'L1_ffn_rhs']


def constants():
    import numpy as np
    f = np.float32
    order = np.concatenate([np.arange(a, P, s) for a, s in ((0, 8), (4, 8), (2, 4), (1, 2))])
    inv_freq = f(1.0) / np.power(f(10000.0), np.arange(0, DK, 2, dtype=f) / f(DK)).astype(f)
    angle = np.outer(np.arange(P, dtype=f), inv_freq).astype(f)
    pair = (np.arange(P) % DK) // 2
    cos, sin = np.cos(angle).astype(f)[:, pair].T, np.sin(angle).astype(f)[:, pair].T
    sin = sin * np.where(np.arange(P) % 2 == 0, f(-1), f(1))[:, None]
    t = np.zeros((P, C_ALL), f)
    t[:, C_ID:C_ID + P] = np.eye(P, dtype=f)
    t[:, C_COS:C_COS + P], t[:, C_COS + P:C_COS + 2 * P] = cos * f(SCALE), cos[:, order]
    t[:, C_SIN:C_SIN + P], t[:, C_SIN + P:C_SIN + 2 * P] = sin * f(SCALE), sin[:, order]
    t[np.arange(P), C_MASK + np.arange(P) // DK % GROUP] = 1.0
    return t


def kernel(**inputs):
    import numpy as _np
    import concourse.bacc as _bacc
    from concourse import mybir as _mybir
    from concourse.bass_utils import run_bass_kernel_spmd as _run

    nc = _bacc.Bacc("TRN2", target_bir_lowering=False, num_devices=1)
    arrays = {f"in_{n}_dram": _np.ascontiguousarray(inputs[n]) for n in _INS}
    arrays["constants_dram"] = constants()
    args = [nc.dram_tensor(n, a.shape, _mybir.dt.from_np(a.dtype), kind="ExternalInput").ap() for n, a in arrays.items()]
    shape = arrays["in_x_dram"].shape
    out = nc.dram_tensor("out_dram", shape, _mybir.dt.float32, kind="ExternalOutput").ap()
    build(nc, *args, out)
    r = _run(nc, [arrays], core_ids=[0])
    return r.results[0]["out_dram"]
```
